# Optimizing a Trainium2 kernel written in Bass

```python
import numpy as np
import jax
import jax.numpy as jnp

def _softmax(x, axis=-1):
    return jax.nn.softmax(x, axis=axis)

def _gelu(x):
    return jax.nn.gelu(x, approximate=True)

def _silu(x):
    return jax.nn.silu(x)

def _sigmoid(x):
    return jax.nn.sigmoid(x)

def _layernorm(x, axis=-1, eps=1e-05):
    m = jnp.mean(x, axis=axis, keepdims=True)
    v = jnp.var(x, axis=axis, keepdims=True)
    return (x - m) / jnp.sqrt(v + eps)

def _scatter_add(tgt, idx, src, axis=0):
    return tgt.at[idx].add(src)

def _segment_sum(src, seg, n):
    return jax.ops.segment_sum(src, seg, n)
kernel_name = 'mk_adj_ffn_d1_adj_r2_fab8eb'

def setup_inputs(seed: int=0):
    np.random.seed(seed)
    _w = jnp.asarray

    def _rec_inputs():
        import jax
        import jax.numpy as jnp
        _gk = jax.random.key(seed)
        x = -0.001003 + 1 * jax.random.normal(jax.random.fold_in(_gk, 1), (4096, 128), jnp.float32)
        _w = (1.0 + jnp.arange(4096, dtype=jnp.float32)) ** (-0.5)
        _w = _w / _w.mean()
        _pij = jnp.clip(0.00390625 * _w[:, None] * _w[None, :], 0.0, 1.0)
        _a = jax.random.uniform(jax.random.fold_in(_gk, 2), (4096, 4096)) < _pij
        _af = _a.astype(jnp.float32)
        _af = _af * jax.random.uniform(jax.random.fold_in(_gk, 3), (4096, 4096), jnp.float32, 0.05, 0.999999)
        adj = _af
        return (x, adj)
    x, adj = _rec_inputs()

    def _L0_gnn_setup():
        import jax, jax.numpy as jnp
        import numpy as np
        N = 3072
        HID = 128
        T = 350
        DENSITY = 0.05
        key = jax.random.key(seed)
        k1, k2, k3, k4, k5, k6 = jax.random.split(key, 6)
        h = jax.random.normal(k1, (N, HID), dtype=jnp.float32)
        a = jax.random.uniform(k2, (N, N), dtype=jnp.float32)
        mask = jax.random.uniform(k3, (N, N)) < DENSITY
        adj = jnp.where(mask, a, 0.0)
        simlar = jax.random.normal(k4, (N, N), dtype=jnp.float32)
        s = 1.0 / np.sqrt(HID)
        W_proj = jax.random.uniform(k5, (HID, HID), minval=-s, maxval=s, dtype=jnp.float32)
        b_proj = jnp.zeros((HID,), dtype=jnp.float32)
        W_gcn = jax.random.uniform(k6, (HID, HID), minval=-s, maxval=s, dtype=jnp.float32)
        b_gcn = jnp.zeros((HID,), dtype=jnp.float32)
        return {'h': h, 'adj': adj, 'simlar': simlar, 'W_proj': W_proj, 'b_proj': b_proj, 'W_gcn': W_gcn, 'b_gcn': b_gcn}
    _L0_gnn_all = _L0_gnn_setup()
    _L0_gnn_in = {k: v for k, v in _L0_gnn_all.items() if k in ('W_proj', 'b_proj', 'W_gcn', 'b_gcn')}
    del _L0_gnn_all

    def _L0_ffn_setup():
        import jax, jax.numpy as jnp
        import numpy as np
        B, S, D, H, E, K = (8, 4096, 128, 512, 8, 2)
        key = jax.random.key(seed)
        ks = jax.random.split(key, 7)
        s_in = 1.0 / np.sqrt(D)
        s_hid = 1.0 / np.sqrt(H)
        return {'x': jax.random.normal(ks[0], (B, S, D), dtype=jnp.float32), 'Wg': jax.random.uniform(ks[1], (E, D), jnp.float32, -s_in, s_in), 'bg': jax.random.uniform(ks[2], (E,), jnp.float32, -s_in, s_in), 'W1': jax.random.uniform(ks[3], (E, H, D), jnp.float32, -s_in, s_in), 'b1': jax.random.uniform(ks[4], (E, H), jnp.float32, -s_in, s_in), 'W2': jax.random.uniform(ks[5], (E, D, H), jnp.float32, -s_hid, s_hid), 'b2': jax.random.uniform(ks[6], (E, D), jnp.float32, -s_hid, s_hid)}
    _L0_ffn_all = _L0_ffn_setup()
    _L0_ffn_in = {k: v for k, v in _L0_ffn_all.items() if k in ('Wg', 'bg', 'W1', 'b1', 'W2', 'b2')}
    del _L0_ffn_all
    return {'x': x, 'adj': adj, 'L0_gnn_W_proj': _L0_gnn_in['W_proj'], 'L0_gnn_b_proj': _L0_gnn_in['b_proj'], 'L0_gnn_W_gcn': _L0_gnn_in['W_gcn'], 'L0_gnn_b_gcn': _L0_gnn_in['b_gcn'], 'L0_ffn_Wg': _L0_ffn_in['Wg'], 'L0_ffn_bg': _L0_ffn_in['bg'], 'L0_ffn_W1': _L0_ffn_in['W1'], 'L0_ffn_b1': _L0_ffn_in['b1'], 'L0_ffn_W2': _L0_ffn_in['W2'], 'L0_ffn_b2': _L0_ffn_in['b2']}

def reference(x, adj, L0_gnn_W_proj, L0_gnn_b_proj, L0_gnn_W_gcn, L0_gnn_b_gcn, L0_ffn_Wg, L0_ffn_bg, L0_ffn_W1, L0_ffn_b1, L0_ffn_W2, L0_ffn_b2):
    import jax
    import jax.numpy as jnp

    def _L0_gnn_ref(h, adj, simlar, W_proj, b_proj, W_gcn, b_gcn):
        import jax, jax.numpy as jnp
        import numpy as np
        N = 3072
        HID = 128
        T = 350
        DENSITY = 0.05
        sim = jnp.tanh(adj * simlar)
        filt = sim * (adj > 0).astype(sim.dtype)
        vals, idx = jax.lax.top_k(filt, T)
        nnz = jnp.sum(filt != 0, axis=1)
        keep = jnp.arange(T)[None, :] < nnz[:, None]
        rows = jnp.arange(filt.shape[0])[:, None]
        new_adj = jnp.zeros_like(filt).at[rows, idx].set(jnp.where(keep, vals, 0.0))
        h2 = jnp.tanh(h @ W_proj + b_proj)
        feat = jax.nn.relu(new_adj @ (h2 @ W_gcn) + b_gcn)
        return feat

    def _L0_ffn_ref(x, Wg, bg, W1, b1, W2, b2):
        import jax, jax.numpy as jnp
        import numpy as np
        B, S, D, H, E, K = (8, 4096, 128, 512, 8, 2)
        gate_scores = jnp.einsum('bsd,ed->bse', x, Wg) + bg
        topk_scores, topk_idx = jax.lax.top_k(gate_scores, K)
        topk_probs = jax.nn.softmax(topk_scores, axis=-1)
        combine = jnp.sum(topk_probs[..., None] * jax.nn.one_hot(topk_idx, E, dtype=x.dtype), axis=-2)
        out = jnp.zeros_like(x)
        for e in range(E):
            h = jax.nn.relu(jnp.einsum('bsd,hd->bsh', x, W1[e]) + b1[e])
            y = jnp.einsum('bsh,dh->bsd', h, W2[e]) + b2[e]
            out = out + combine[..., e:e + 1] * y
        return out
    x = x + _L0_gnn_ref(_layernorm(x, axis=-1), adj, adj, L0_gnn_W_proj, L0_gnn_b_proj, L0_gnn_W_gcn, L0_gnn_b_gcn)
    x = x + _L0_ffn_ref(_layernorm(x, axis=-1)[None], L0_ffn_Wg, L0_ffn_bg, L0_ffn_W1, L0_ffn_b1, L0_ffn_W2, L0_ffn_b2)[0]
    return x

_drawn_inputs = setup_inputs


def setup_inputs(seed=0):
    import zlib

    import numpy as np

    out = dict(_drawn_inputs(seed))
    spreads = {'L0_gnn_b_proj': (0.0, 0.1), 'L0_gnn_b_gcn': (0.0, 0.1)}
    factors = {'L0_ffn_b1': 4.119, 'L0_ffn_b2': 3.282}
    for name, (base, spread) in spreads.items():
        noise = np.random.default_rng([zlib.crc32(name.encode()), seed]).standard_normal(out[name].shape)
        drawn = base * np.exp(spread * noise) if base else spread * noise
        out[name] = jnp.asarray(drawn.astype(out[name].dtype))
    for name, factor in factors.items():
        out[name] = (out[name] * factor).astype(out[name].dtype)
    return out
```

```python
import numpy as np
import concourse.bass as bass
from concourse import mybir
from contextlib import ExitStack


def gnn_moe_layer(nc, x, adj_tiles, adj_rows, w_proj, b_proj, w_gcn, b_gcn,
                  w_gate, b_gate, w1, b1, w2, b2, out):
    fp32, bf16, i32 = mybir.dt.float32, mybir.dt.bfloat16, mybir.dt.int32
    ALU, ACT, AX = mybir.AluOpType, mybir.ActivationFunctionType, mybir.AxisListType

    P = 128
    N, D = x.shape
    C = N // P
    TOPK = 350
    EPS = 1e-5
    E, H = b2.shape[0], w1.shape[2]
    HB = H // P
    IW = 512
    NB = N // IW
    CK = 4
    NK = C // CK
    NBUF = 4
    GW = CK * P
    R = 8
    BITS = 30
    SUB = IW // P

    ctx = ExitStack()
    with ctx:
        def sb(name, shape, dt=fp32):
            return ctx.enter_context(nc.sbuf_tensor(name, shape, dt))

        def sem(name):
            return ctx.enter_context(nc.semaphore(name))

        ctx.enter_context(nc.allow_low_precision(reason="counts of at most C are exact"))

        xres = sb("xres", [P, C, D])
        xnorm = sb("xnorm", [P, C, D])
        big_t = sb("big_t", [P, N])
        g_sb = sb("g_sb", [P, C, D])
        w1_sb = sb("w1_sb", [P, E, H])
        w2_sb = sb("w2_sb", [P, E, HB, D])
        abuf = sb("abuf", [P, NBUF, CK, IW])
        tbuf = sb("tbuf", [P, NBUF, CK, IW])
        ind = sb("ind", [P, NBUF, CK, IW], bf16)
        xn2t = tbuf[:, :, :, :].rearrange("p a b c -> p (a b c)")[:, 0:N]
        hid = abuf
        ident = sb("ident", [P, P])
        ones_bf = sb("ones_bf", [P, P], bf16)
        before = sb("before", [P, P], bf16)
        wp_sb = sb("wp_sb", [P, D])
        wg_sb = sb("wg_sb", [P, D])
        bp_sb = sb("bp_sb", [P, 1])
        bg_sb = sb("bg_sb", [P, 1])
        gate_w = sb("gate_w", [P, E])
        gate_b = sb("gate_b", [1, E])
        ones_row = sb("ones_row", [1, P])
        b1_sb = sb("b1_sb", [P, E, HB])
        b2_sb = sb("b2_sb", [E, D])
        h2t = sb("h2t", [P, 2, GW])
        stats = sb("stats", [P, C, 6])
        mean = sb("mean", [P, C])
        var = sb("var", [P, C])
        sd = sb("sd", [P, C])
        rstd = sb("rstd", [P, C])
        tmp = sb("tmp", [P, C])
        rowid = sb("rowid", [P, C], i32)
        rowidf = sb("rowidf", [P, C])
        count = sb("count", [P, C])
        key = sb("key", [P, C])
        keyrow = xnorm[0:1, :, :].rearrange("o c d -> o (c d)")
        keyrow2 = tbuf[0:1, :, :, :].rearrange("o a b c -> o (a b c)")[:, 0:N]
        nflag = sb("nflag", [1, 1])
        nrounds = sb("nrounds", [1, 1], i32)
        top = sb("top", [1, 8])
        ids = sb("ids", [1, 8], i32)
        rowbuf = sb("rowbuf", [P, R, C])
        val = sb("val", [P, R, C])
        thr = sb("thr", [P, R], i32)
        cand = sb("cand", [P, 3, R], i32)
        ge = sb("ge", [P, 3, R, C])
        part = sb("part", [P, 3, R], bf16)
        okk = sb("okk", [P, 3, R])
        step = sb("step", [P, R], i32)
        gt = sb("gt", [P, R, C])
        eq = sb("eq", [P, R, C])
        scan = sb("scan", [P, 2, R, C])
        pair = sb("pair", [P, 2, R], bf16)
        need = sb("need", [P, R])
        fixed = sb("fixed", [P, R])
        scores = sb("scores", [P, C, E])
        masked = sb("masked", [P, C, E])
        onehot1 = sb("onehot1", [P, C, E])
        onehot2 = sb("onehot2", [P, C, E])
        eidx = sb("eidx", [P, C, E])
        eidx_i = sb("eidx_i", [P, C, E], i32)
        m1 = sb("m1", [P, C])
        m2 = sb("m2", [P, C])
        pick = sb("pick", [P, C])
        p1 = sb("p1", [P, C])
        p2 = sb("p2", [P, C])
        comb = sb("comb", [P, C, E])
        comb_t = xnorm[0:E, :, :].rearrange("e c d -> e (c d)")

        bank = [ctx.enter_context(nc.psum_tensor(f"bank{i}", [P, 512], fp32)) for i in range(8)]
        ps_feat, ps_cnt = bank[0:2], bank[2:4]
        ps_t, ps_mm = bank[4:6], bank[6:8]

        s_x = sem("s_x")
        s_w = sem("s_w")
        s_ffw = sem("s_ffw")
        s_const = sem("s_const")
        s_pool = sem("s_pool")
        s_dve = sem("s_dve")
        s_var = sem("s_var")
        s_sd = sem("s_sd")
        s_xn = sem("s_xn")
        s_tr = sem("s_tr")
        s_trc = sem("s_trc")
        s_proj = sem("s_proj")
        s_h2 = sem("s_h2")
        s_gp = sem("s_gp")
        s_g = sem("s_g")
        s_a = [sem(f"s_a{i}") for i in range(NBUF)]
        s_sq = sem("s_sq")
        s_t = sem("s_t")
        s_ind = sem("s_ind")
        s_pe = sem("s_pe")
        s_ev = sem("s_ev")
        s_cnt = sem("s_cnt")
        s_key = sem("s_key")
        s_keyrow = sem("s_keyrow")
        s_nr = sem("s_nr")
        s_ids = sem("s_ids")
        s_rows = sem("s_rows")
        s_fdve = sem("s_fdve")
        s_rsq = sem("s_rsq")
        s_val = sem("s_val")
        s_part = sem("s_part")
        s_tot = sem("s_tot")
        s_keep = sem("s_keep")
        s_fmm = sem("s_fmm")
        s_fix = sem("s_fix")
        s_wr = sem("s_wr")
        s_fixed = sem("s_fixed")
        s_ft = sem("s_ft")
        s_x2 = sem("s_x2")
        s_gate = sem("s_gate")
        s_diff = sem("s_diff")
        s_exp = sem("s_exp")
        s_comb = sem("s_comb")
        s_ct = sem("s_ct")
        s_ctc = sem("s_ctc")
        s_b2 = sem("s_b2")
        s_acc0 = sem("s_acc0")
        s_h = sem("s_h")
        s_relu = sem("s_relu")
        s_y = sem("s_y")
        s_acc = sem("s_acc")
        s_spare = sem("s_spare")
        s_out = sem("s_out")

        block = ctx.enter_context(nc.Block())

        @block.sync
        def _(sp):
            sp.dma_start(xres[:, :, :], x.rearrange("(p c) d -> p c d", p=P)).then_inc(s_x, 16)

            def load_block(ib, first=False):
                for k in range(NK):
                    if not (first and k < NBUF):
                        sp.wait_ge(s_t, ib * NK + k - NBUF + 1)
                    sp.dma_start(abuf[:, k % NBUF, :, :], adj_tiles[bass.ds(ib, 1), k, :, :, :]
                                 .rearrange("o p c i -> p (o c) i")).then_inc(s_a[k % NBUF], 16)

            load_block(0, first=True)
            with sp.Fori(1, NB) as ib:
                load_block(ib)

            sp.wait_ge(s_key, 1)
            sp.dma_start(keyrow[0:1, :].rearrange("o (p t) -> o p t", p=P), key[:, :].rearrange("p (o t) -> p o t", o=1)
                         ).then_inc(s_keyrow, 16)
            sp.wait_ge(s_nr, 1)
            rounds = sp.value_load(nrounds[0:1, 0:1], min_val=1, max_val=N // R)
            with sp.Fori(0, rounds) as r:
                sp.wait_ge(s_ids, r + 1)
                for q in range(R):
                    if q == 0:
                        sp.sem_inc(s_spare, 1)
                    row = sp.value_load(ids[0:1, q:q + 1], min_val=0, max_val=N - 1)
                    sp.dma_start(rowbuf[:, q, :], adj_rows[bass.ds(row, 1), :]
                                 .rearrange("o (p c) -> p (o c)", p=P)).then_inc(s_rows, 16)

            sp.wait_ge(s_acc, NB * E)
            sp.dma_start(out.rearrange("(p c) d -> p c d", p=P), xres[:, :, :]).then_inc(s_out, 16)
            sp.wait_ge(s_out, 16)

        @block.gpsimd
        def _(pool):
            pool.dma_start(wp_sb[:, :], w_proj).then_inc(s_w, 16)
            pool.dma_start(wg_sb[:, :], w_gcn).then_inc(s_w, 16)
            pool.dma_start(bp_sb[:, :], b_proj.rearrange("(p o) -> p o", o=1)).then_inc(s_w, 16)
            pool.dma_start(bg_sb[:, :], b_gcn.rearrange("(p o) -> p o", o=1)).then_inc(s_w, 16)
            pool.memset(ident[:, :], 0.0).then_inc(s_pool, 1)
            pool.memset(ones_bf[:, :], 1.0).then_inc(s_pool, 1)
            pool.memset(ones_row[:, :], 1.0).then_inc(s_pool, 1)
            pool.wait_ge(s_pool, 3)
            pool.affine_select(out=ident[:, :], in_=ident[:, :], compare_op=ALU.not_equal, fill=1.0, base=0,
                               pattern=[[-1, P]], channel_multiplier=1).then_inc(s_const, 1)
            pool.affine_select(out=before[:, :], in_=ones_bf[:, :], compare_op=ALU.is_ge, fill=0.0, base=-1,
                               pattern=[[1, P]], channel_multiplier=-1).then_inc(s_const, 1)
            pool.iota(rowid[:, :], [[P, C]], base=1, channel_multiplier=1).then_inc(s_const, 1)
            pool.iota(eidx_i[:, :, :], [[0, C], [-1, E]], base=E, channel_multiplier=0).then_inc(s_const, 1)
            pool.dma_start(w1_sb[:, :, :], w1).then_inc(s_ffw, 16)
            pool.dma_start(w2_sb[:, :, :, :], w2).then_inc(s_ffw, 16)
            pool.dma_start(b1_sb[:, :, :], b1).then_inc(s_ffw, 16)
            pool.dma_start(b2_sb[:, :], b2).then_inc(s_ffw, 16)
            pool.dma_start(gate_w[:, :], w_gate).then_inc(s_ffw, 16)
            pool.dma_start(gate_b[:, :], b_gate.rearrange("(o e) -> o e", o=1)).then_inc(s_ffw, 16)

        @block.vector
        def _(dve):
            chain = [0]

            def link(ins):
                chain[0] += 1
                ins.then_inc(s_dve, 1)
                dve.wait_ge(s_dve, chain[0])

            def layernorm_rows(which):
                for c in range(C):
                    last = dve.bn_stats(stats[:, c, :], xres[:, c, :])
                link(last)
                link(dve.tensor_tensor(mean[:, :], stats[:, :, 1], stats[:, :, 4], ALU.add))
                link(dve.tensor_tensor(tmp[:, :], stats[:, :, 1], stats[:, :, 4], ALU.subtract))
                link(dve.tensor_tensor(var[:, :], stats[:, :, 2], stats[:, :, 5], ALU.add))
                link(dve.tensor_tensor(tmp[:, :], tmp[:, :], tmp[:, :], ALU.mult))
                link(dve.tensor_scalar(mean[:, :], mean[:, :], 0.5, None, ALU.mult))
                link(dve.tensor_scalar(tmp[:, :], tmp[:, :], 0.25, EPS, ALU.mult, ALU.add))
                dve.scalar_tensor_tensor(var[:, :], var[:, :], 1.0 / D, tmp[:, :], ALU.mult, ALU.add
                                         ).then_inc(s_var, 1)
                dve.wait_ge(s_sd, which + 1)
                link(dve.reciprocal(rstd[:, :], sd[:, :]))
                link(dve.tensor_tensor(tmp[:, :], rstd[:, :], rstd[:, :], ALU.mult))
                link(dve.tensor_tensor(tmp[:, :], tmp[:, :], var[:, :], ALU.mult))
                link(dve.tensor_scalar(tmp[:, :], tmp[:, :], -0.5, 1.5, ALU.mult, ALU.add))
                link(dve.tensor_tensor(rstd[:, :], rstd[:, :], tmp[:, :], ALU.mult))
                for c in range(C):
                    ins = dve.tensor_scalar(xnorm[:, c, :], xres[:, c, :], mean[:, c:c + 1], rstd[:, c:c + 1],
                                            ALU.subtract, ALU.mult)
                    if c % CK == CK - 1:
                        ins.then_inc(s_xn, 1)

            dve.wait_ge(s_x, 16)
            layernorm_rows(0)
            for g in range(NK):
                dve.wait_ge(s_tr, g + 1)
                dve.tensor_copy(big_t[:, g * GW:(g + 1) * GW], ps_t[g % 2][:, :]).then_inc(s_trc, 1)
                if g:
                    dve.wait_ge(s_gp, g)
                    dve.tensor_copy(g_sb[:, (g - 1) * CK:g * CK, :],
                                    ps_feat[(g - 1) % 2][:, :].rearrange("p (c d) -> p c d", c=CK)).then_inc(s_g, 1)
            dve.wait_ge(s_gp, NK)
            dve.tensor_copy(g_sb[:, (NK - 1) * CK:, :],
                            ps_feat[(NK - 1) % 2][:, :].rearrange("p (c d) -> p c d", c=CK)).then_inc(s_g, 1)

            def square_block(pb, first=False):
                for m in range(2 * NK):
                    n = pb * 2 * NK + m
                    b = m % NBUF
                    dve.wait_ge(s_a[b], (pb * (2 * NK // NBUF) + m // NBUF + 1) * 16)
                    dve.scalar_tensor_tensor(abuf[:, b, :, :], abuf[:, b, :, :], 0.0, abuf[:, b, :, :],
                                             ALU.max, ALU.mult).then_inc(s_sq, 1)
                    indicate(n - 1, (m - 1) % NBUF, first and m <= NBUF, skip=first and m == 0)
                    if m % NK == 0 and not (first and m == 0):
                        counts_out(pb * 2 + m // NK - 1, (m // NK - 1) % 2)

            def indicate(n, b, fresh, skip=False):
                if skip:
                    return
                dve.wait_ge(s_t, n + 1)
                if not fresh:
                    dve.wait_ge(s_pe, n - NBUF + 1)
                dve.tensor_scalar(ind[:, b, :, :], tbuf[:, b, :, :], 0.0, None, ALU.is_gt).then_inc(s_ind, 1)

            def counts_out(ib, parity):
                dve.wait_ge(s_pe, (ib + 1) * NK)
                dve.tensor_copy(count[:, bass.ds(ib * SUB, SUB)], ps_cnt[parity][:, 0:SUB]).then_inc(s_cnt, 1)

            square_block(0, first=True)
            with dve.Fori(1, NB // 2) as pb:
                square_block(pb)
            indicate(NB * NK - 1, NBUF - 1, False)
            counts_out(NB - 1, 1)
            dve.wait_ge(s_cnt, NB)

            dve.wait_ge(s_const, 4)
            link(dve.tensor_copy(rowidf[:, :], rowid[:, :]))
            link(dve.tensor_scalar(key[:, :], count[:, :], float(TOPK), None, ALU.is_gt))
            dve.tensor_tensor(key[:, :], key[:, :], rowidf[:, :], ALU.mult).then_inc(s_key, 1)
            dve.wait_ge(s_keyrow, 16)
            link(dve.tensor_scalar(keyrow2[:, :], keyrow[:, :], 0.0, None, ALU.is_gt))
            link(dve.tensor_reduce(nflag[:, :], keyrow2[:, :], AX.X, ALU.add))
            dve_chain = dve.tensor_scalar(nflag[:, :], nflag[:, :], 1.0 / R, 0.5 - 0.5 / R, ALU.mult, ALU.add)
            link(dve_chain)
            dve.tensor_scalar(nrounds[:, :], nflag[:, :], 1.0, None, ALU.max).then_inc(s_nr, 1)
            dve.wait_ge(s_nr, 1)
            rounds = dve.value_load(nrounds[0:1, 0:1], min_val=1, max_val=N // R)
            CHAIN = 2 + 6 * (BITS // 2) + 3 + 5 + 5 + R
            TOTS = BITS // 2 + 1

            with dve.Fori(0, rounds) as r:
                links = [0]

                def rlink(ins):
                    links[0] += 1
                    ins.then_inc(s_fdve, 1)
                    dve.wait_ge(s_fdve, r * CHAIN + links[0])

                rlink(dve.max(top[:, :], keyrow[:, :]))
                dve.tensor_scalar(ids[:, :], top[:, :], -1.0, 0.0, ALU.add, ALU.max).then_inc(s_ids, 1)
                dve.match_replace(keyrow[:, :], top[:, :], keyrow[:, :], 0.0)
                rlink(dve.memset(thr[:, :], 0))
                dve.wait_ge(s_rows, (r + 1) * 16 * R)
                dve.scalar_tensor_tensor(val[:, :, :], rowbuf[:, :, :], 0.0, rowbuf[:, :, :], ALU.max, ALU.mult
                                         ).then_inc(s_rsq, 1)
                dve.wait_ge(s_val, r + 1)
                for b in range(BITS // 2):
                    sh = BITS - 2 - 2 * b
                    for k in range(3):
                        last = dve.tensor_scalar(cand[:, k, :], thr[:, :], (k + 1) << sh, None, ALU.bitwise_or)
                    rlink(last)
                    for k in range(3):
                        last = dve.tensor_tensor(
                            ge[:, k, :, :], val[:, :, :],
                            cand[:, k, :].bitcast(fp32).rearrange("p (r o) -> p r o", o=1).to_broadcast([P, R, C]),
                            ALU.is_ge)
                    rlink(last)
                    dve.tensor_reduce(part[:, :, :], ge[:, :, :, :], AX.X, ALU.add).then_inc(s_part, 1)
                    dve.wait_ge(s_tot, r * TOTS + b + 1)
                    rlink(dve.tensor_scalar(okk[:, :, :], ps_mm[0][:, 0:3 * R].rearrange("p (k r) -> p k r", k=3),
                                            float(TOPK), None, ALU.is_ge))
                    rlink(dve.tensor_reduce(step[:, :], okk[:, :, :].rearrange("p k r -> p r k"), AX.X, ALU.add))
                    rlink(dve.tensor_scalar(step[:, :], step[:, :], sh, None, ALU.logical_shift_left))
                    rlink(dve.tensor_tensor(thr[:, :], thr[:, :], step[:, :], ALU.bitwise_or))
                tb = thr[:, :].bitcast(fp32).rearrange("p (r o) -> p r o", o=1).to_broadcast([P, R, C])
                rlink(dve.tensor_tensor(gt[:, :, :], val[:, :, :], tb, ALU.is_gt))
                rlink(dve.tensor_tensor(eq[:, :, :], val[:, :, :], tb, ALU.is_equal))
                rlink(dve.tensor_reduce(pair[:, 0, :], gt[:, :, :], AX.X, ALU.add))
                dve.tensor_reduce(pair[:, 1, :], eq[:, :, :], AX.X, ALU.add).then_inc(s_part, 1)
                src = eq[:, :, :]
                for s in range(5):
                    dst = scan[:, s % 2, :, :]
                    w = 1 << s
                    dve.tensor_copy(dst[:, :, 0:w], src[:, :, 0:w])
                    rlink(dve.tensor_tensor(dst[:, :, w:C], src[:, :, w:C], src[:, :, 0:C - w], ALU.add))
                    src = dst
                dve.wait_ge(s_tot, (r + 1) * TOTS)
                rlink(dve.tensor_scalar(need[:, :], ps_mm[0][:, 0:R], -1.0, float(TOPK), ALU.mult, ALU.add))
                rlink(dve.tensor_tensor(need[:, :], need[:, :], ps_mm[0][:, R:2 * R], ALU.subtract))
                rlink(dve.tensor_tensor(src, src, need[:, :].rearrange("p (r o) -> p r o", o=1)
                                        .to_broadcast([P, R, C]), ALU.is_le))
                rlink(dve.tensor_tensor(eq[:, :, :], eq[:, :, :], src, ALU.mult))
                rlink(dve.tensor_tensor(gt[:, :, :], gt[:, :, :], eq[:, :, :], ALU.add))
                dve.tensor_tensor(gt[:, :, :], gt[:, :, :], val[:, :, :], ALU.mult).then_inc(s_keep, 1)
                dve.wait_ge(s_fix, r + 1)
                dve.sem_inc(s_spare, 1)
                rows = [dve.value_load(ids[0:1, q:q + 1], min_val=0, max_val=N - 1) for q in range(R)]
                for q in range(R):
                    rlink(dve.tensor_copy(big_t[:, bass.ds(rows[q], 1)], fixed[:, q:q + 1]))
                assert links[0] == CHAIN, links
            dve.memset(tmp[:, :], 0.0).then_inc(s_fixed, 1)

            for g in range(NK):
                dve.wait_ge(s_ft, g + 1)
                dve.tensor_tensor(xres[:, g * CK:(g + 1) * CK, :], xres[:, g * CK:(g + 1) * CK, :],
                                  ps_t[g % 2][:, :].rearrange("p (c d) -> p c d", c=CK), ALU.add).then_inc(s_x2, 1)
            dve.wait_ge(s_x2, NK)
            layernorm_rows(1)
            for g in range(NK):
                dve.wait_ge(s_tr, NK + g + 1)
                dve.tensor_copy(xn2t[:, g * GW:(g + 1) * GW], ps_t[g % 2][:, :]).then_inc(s_trc, 1)
            link(dve.tensor_copy(eidx[:, :, :], eidx_i[:, :, :]))
            dve.wait_ge(s_gate, 1)
            link(dve.tensor_copy(scores[:, :, :], ps_mm[0][:, 0:C * E].rearrange("p (c e) -> p c e", e=E)))

            def spread(v):
                return v[:, :].rearrange("p (c o) -> p c o", o=1).to_broadcast([P, C, E])

            def first_of_max(src, m, onehot):
                link(dve.tensor_reduce(m[:, :], src, AX.X, ALU.max))
                link(dve.tensor_tensor(onehot[:, :, :], src, spread(m), ALU.is_equal))
                link(dve.tensor_tensor(onehot[:, :, :], onehot[:, :, :], eidx[:, :, :], ALU.mult))
                link(dve.tensor_reduce(pick[:, :], onehot[:, :, :], AX.X, ALU.max))
                link(dve.tensor_tensor(onehot[:, :, :], eidx[:, :, :], spread(pick), ALU.is_equal))

            first_of_max(scores[:, :, :], m1, onehot1)
            link(dve.scalar_tensor_tensor(masked[:, :, :], onehot1[:, :, :], -3.0e38, scores[:, :, :],
                                          ALU.mult, ALU.add))
            first_of_max(masked[:, :, :], m2, onehot2)
            dve.tensor_tensor(m2[:, :], m2[:, :], m1[:, :], ALU.subtract).then_inc(s_diff, 1)
            dve.wait_ge(s_exp, 1)
            link(dve.tensor_scalar(p1[:, :], p2[:, :], 1.0, None, ALU.add))
            link(dve.reciprocal(p1[:, :], p1[:, :]))
            link(dve.tensor_tensor(p2[:, :], p2[:, :], p1[:, :], ALU.mult))
            link(dve.tensor_tensor(onehot1[:, :, :], onehot1[:, :, :], spread(p1), ALU.mult))
            link(dve.tensor_tensor(onehot2[:, :, :], onehot2[:, :, :], spread(p2), ALU.mult))
            dve.tensor_tensor(comb[:, :, :], onehot1[:, :, :], onehot2[:, :, :], ALU.add).then_inc(s_comb, 1)
            dve.wait_ge(s_comb, 1)

            for g in range(NK):
                dve.wait_ge(s_ct, g + 1)
                dve.tensor_copy(comb_t[:, g * GW:(g + 1) * GW], ps_t[0][0:E, :]).then_inc(s_ctc, 1)
                dve.wait_ge(s_b2, g + 1)
                dve.tensor_tensor(xres[:, g * CK:(g + 1) * CK, :], xres[:, g * CK:(g + 1) * CK, :],
                                  ps_t[1][:, :].rearrange("p (c d) -> p c d", c=CK), ALU.add).then_inc(s_acc0, 1)
            dve.wait_ge(s_acc0, NK)
            with dve.Fori(0, NB) as g:
                for e in range(E):
                    dve.wait_ge(s_y, g * E + e + 1)
                    if e:
                        dve.wait_ge(s_acc, g * E + e)
                    for cc in range(CK):
                        last = dve.scalar_tensor_tensor(
                            xres[:, bass.ds(g * CK + cc, 1), :].rearrange("p o d -> p (o d)"),
                            ps_feat[e % 2][:, cc * P:(cc + 1) * P],
                            comb[:, bass.ds(g * CK + cc, 1), e],
                            xres[:, bass.ds(g * CK + cc, 1), :].rearrange("p o d -> p (o d)"),
                            ALU.mult, ALU.add)
                    last.then_inc(s_acc, 1)

        @block.scalar
        def _(act):
            act.wait_ge(s_var, 1)
            act.activation(sd[:, :], var[:, :], ACT.Sqrt).then_inc(s_sd, 1)
            act.wait_ge(s_w, 64)
            for g in range(NK):
                act.wait_ge(s_proj, g + 1)
                if g >= 2:
                    act.wait_ge(s_gp, g - 1)
                act.activation(h2t[:, g % 2, :], ps_mm[g % 2][:, :], ACT.Tanh, bias=bp_sb[:, 0:1]).then_inc(s_h2, 1)

            def tanh_block(pb, first=False):
                for m in range(2 * NK):
                    n = pb * 2 * NK + m
                    b = m % NBUF
                    act.wait_ge(s_sq, n + 1)
                    if not (first and m < NBUF):
                        act.wait_ge(s_pe, n - NBUF + 1)
                        act.wait_ge(s_ind, n - NBUF + 1)
                    act.activation(tbuf[:, b, :, :], abuf[:, b, :, :], ACT.Tanh).then_inc(s_t, 1)
                    if m % NK == 1 and not (first and m == 1):
                        feat_out(pb * 2 + m // NK - 1, (m // NK - 1) % 2)

            def feat_out(ib, parity):
                act.wait_ge(s_pe, (ib + 1) * NK)
                act.activation(big_t[:, bass.ds(ib * IW, IW)], ps_feat[parity][:, :], ACT.Relu,
                               bias=bg_sb[:, 0:1]).then_inc(s_ev, 1)

            act.wait_ge(s_proj, NK)
            tanh_block(0, first=True)
            with act.Fori(1, NB // 2) as pb:
                tanh_block(pb)
            feat_out(NB - 1, 1)
            act.wait_ge(s_nr, 1)
            rounds = act.value_load(nrounds[0:1, 0:1], min_val=1, max_val=N // R)
            with act.Fori(0, rounds) as r:
                act.wait_ge(s_rsq, r + 1)
                act.activation(val[:, :, :], val[:, :, :], ACT.Tanh).then_inc(s_val, 1)
                act.wait_ge(s_fmm, r + 1)
                act.activation(fixed[:, :], ps_mm[1][:, 0:R], ACT.Relu, bias=bg_sb[:, 0:1]).then_inc(s_fix, 1)
            act.wait_ge(s_var, 2)
            act.activation(sd[:, :], var[:, :], ACT.Sqrt).then_inc(s_sd, 1)
            act.wait_ge(s_diff, 1)
            act.activation(p2[:, :], m2[:, :], ACT.Exp).then_inc(s_exp, 1)
            act.wait_ge(s_ffw, 96)

            def relu_group(g, first):
                for e in range(E):
                    for hb in range(HB):
                        n = g * E * HB + e * HB + hb
                        act.wait_ge(s_h, n + 1)
                        if not (first and e < 2) and hb == 0:
                            act.wait_ge(s_y, g * E + e - 1)
                        act.activation(hid[:, (e % 2) * 2 + hb // 2, hb % 2, :],
                                       ps_mm[hb % 2][:, :], ACT.Relu, bias=b1_sb[:, e, hb:hb + 1]).then_inc(s_relu, 1)

            relu_group(0, True)
            with act.Fori(1, NB) as g:
                relu_group(g, False)

        @block.tensor
        def _(pe):
            def transpose_group(src, g, done, free):
                if free is not None:
                    pe.wait_ge(*free)
                for cc in range(CK):
                    last = pe.transpose(ps_t[g % 2][:, cc * P:(cc + 1) * P], src(g * CK + cc), ident[:, :])
                last.then_inc(done, 1)

            pe.wait_ge(s_const, 1)
            pe.wait_ge(s_w, 64)

            def project(g):
                pe.wait_ge(s_trc, g + 1)
                if g >= 2:
                    pe.wait_ge(s_h2, g - 1)
                pe.matmul(ps_mm[g % 2][:, :], wp_sb[:, :], big_t[:, g * GW:(g + 1) * GW],
                          start=True, stop=True).then_inc(s_proj, 1)

            def make_g(g):
                pe.wait_ge(s_h2, g + 1)
                if g >= 2:
                    pe.wait_ge(s_g, g - 1)
                for cc in range(CK):
                    last = pe.matmul(ps_feat[g % 2][:, cc * P:(cc + 1) * P], h2t[:, g % 2, cc * P:(cc + 1) * P],
                                     wg_sb[:, :], start=True, stop=True)
                last.then_inc(s_gp, 1)

            for g in range(NK):
                pe.wait_ge(s_xn, g + 1)
                transpose_group(lambda c: xnorm[:, c, :], g, s_tr, (s_trc, g - 1) if g >= 2 else None)
                project(g)
                if g:
                    make_g(g - 1)
            make_g(NK - 1)
            pe.wait_ge(s_g, NK)

            def gnn_blocks(pb, first=False):
                for m in range(2 * NK):
                    n = pb * 2 * NK + m
                    b, half, k = m % NBUF, m // NK, m % NK
                    if k == 0 and not first:
                        pe.wait_ge(s_ev, pb * 2 + half - 1)
                        pe.wait_ge(s_cnt, pb * 2 + half - 1)
                    pe.wait_ge(s_t, n + 1)
                    for cc in range(CK):
                        c = k * CK + cc
                        pe.matmul(ps_feat[half][:, :], g_sb[:, c, :], tbuf[:, b, cc, :],
                                  start=(c == 0), stop=(c == C - 1))
                    pe.wait_ge(s_ind, n + 1)
                    for cc in range(CK):
                        c = k * CK + cc
                        for s in range(SUB):
                            last = pe.matmul(ps_cnt[half][:, s:s + 1], ind[:, b, cc, s * P:(s + 1) * P],
                                             ones_bf[:, 0:1], start=(c == 0 and s == 0), stop=(c == C - 1),
                                             skip_group_check=True)
                    last.then_inc(s_pe, 1)

            gnn_blocks(0, first=True)
            with pe.Fori(1, NB // 2) as pb:
                gnn_blocks(pb)

            pe.wait_ge(s_const, 4)
            pe.wait_ge(s_nr, 1)
            rounds = pe.value_load(nrounds[0:1, 0:1], min_val=1, max_val=N // R)
            TOTS = BITS // 2 + 1
            with pe.Fori(0, rounds) as r:
                for b in range(BITS // 2):
                    pe.wait_ge(s_part, r * TOTS + b + 1)
                    pe.matmul(ps_mm[0][:, 0:3 * R], ones_bf[:, :], part[:, :, :], start=True, stop=True
                              ).then_inc(s_tot, 1)
                pe.wait_ge(s_part, (r + 1) * TOTS)
                pe.matmul(ps_mm[0][:, 0:R], ones_bf[:, :], pair[:, 0, :], start=True, stop=True)
                pe.matmul(ps_mm[0][:, R:2 * R], before[:, :], pair[:, 1, :], start=True, stop=True
                          ).then_inc(s_tot, 1)
                pe.wait_ge(s_keep, r + 1)
                for c in range(C):
                    last = pe.matmul(ps_mm[1][:, 0:R], g_sb[:, c, :], gt[:, :, c], start=(c == 0), stop=(c == C - 1))
                last.then_inc(s_fmm, 1)

            pe.wait_ge(s_ev, NB)
            pe.wait_ge(s_fixed, 1)
            for g in range(NK):
                transpose_group(lambda c: big_t[:, c::C], g, s_ft, (s_x2, g - 1) if g >= 2 else None)
            for g in range(NK):
                pe.wait_ge(s_xn, NK + g + 1)
                transpose_group(lambda c: xnorm[:, c, :], g, s_tr, (s_trc, NK + g - 1))
            pe.wait_ge(s_trc, 2 * NK)
            pe.wait_ge(s_ffw, 96)
            for c in range(C):
                pe.matmul(ps_mm[0][:, c * E:(c + 1) * E], xn2t[:, c * P:(c + 1) * P], gate_w[:, :],
                          start=True, stop=False)
                last = pe.matmul(ps_mm[0][:, c * E:(c + 1) * E], ones_row[0:1, :], gate_b[0:1, :],
                                 start=False, stop=True)
            last.then_inc(s_gate, 1)
            pe.wait_ge(s_comb, 1)

            for g in range(NK):
                if g:
                    pe.wait_ge(s_ctc, g)
                for cc in range(CK):
                    last = pe.transpose(ps_t[0][0:E, cc * P:(cc + 1) * P], comb[:, g * CK + cc, :], ident[:, :])
                last.then_inc(s_ct, 1)
                if g:
                    pe.wait_ge(s_acc0, g)
                pe.wait_ge(s_ctc, g + 1)
                for cc in range(CK):
                    last = pe.matmul(ps_t[1][:, cc * P:(cc + 1) * P], comb_t[:, (g * CK + cc) * P:(g * CK + cc + 1) * P],
                                     b2_sb[:, :], start=True, stop=True)
                last.then_inc(s_b2, 1)

            def ffn_group(g, first):
                def hidden(e):
                    for hb in range(HB):
                        n = g * E * HB + e * HB + hb
                        if not (first and e == 0 and hb < 2):
                            pe.wait_ge(s_relu, n - 1)
                        pe.matmul(ps_mm[hb % 2][:, :], w1_sb[:, e, hb * P:(hb + 1) * P],
                                  xn2t[:, bass.ds(g * GW, GW)], start=True, stop=True).then_inc(s_h, 1)

                def outputs(e):
                    pe.wait_ge(s_relu, (g * E + e + 1) * HB)
                    if not (first and e < 2):
                        pe.wait_ge(s_acc, g * E + e - 1)
                    for cc in range(CK):
                        for hb in range(HB):
                            last = pe.matmul(ps_feat[e % 2][:, cc * P:(cc + 1) * P],
                                             hid[:, (e % 2) * 2 + hb // 2, hb % 2, cc * P:(cc + 1) * P],
                                             w2_sb[:, e, hb, :], start=(hb == 0), stop=(hb == HB - 1))
                    last.then_inc(s_y, 1)

                hidden(0)
                for e in range(E):
                    if e + 1 < E:
                        hidden(e + 1)
                    outputs(e)

            ffn_group(0, True)
            with pe.Fori(1, NB) as g:
                ffn_group(g, False)


def kernel(**inputs):
    import concourse.bacc as bacc
    from concourse.bass_utils import run_bass_kernel_spmd

    P, IW, CK = 128, 512, 4
    a = {k: np.asarray(v) for k, v in inputs.items()}
    adj = a["adj"]
    N = adj.shape[0]
    C = N // P
    w1, w2, b1 = a["L0_ffn_W1"], a["L0_ffn_W2"], a["L0_ffn_b1"]
    E, H, D = w1.shape
    laid = {
        "x": a["x"],
        "adj_tiles": adj.reshape(N // IW, IW, P, C // CK, CK).transpose(0, 3, 2, 4, 1),
        "adj_rows": adj,
        "w_proj": a["L0_gnn_W_proj"], "b_proj": a["L0_gnn_b_proj"],
        "w_gcn": a["L0_gnn_W_gcn"], "b_gcn": a["L0_gnn_b_gcn"],
        "w_gate": a["L0_ffn_Wg"].T, "b_gate": a["L0_ffn_bg"],
        "w1": w1.transpose(2, 0, 1),
        "b1": b1.reshape(E, H // P, P).transpose(2, 0, 1),
        "w2": w2.reshape(E, D, H // P, P).transpose(3, 0, 2, 1),
        "b2": a["L0_ffn_b2"],
    }
    nc = bacc.Bacc("TRN2", target_bir_lowering=False, num_devices=1)
    arrays, args = {}, []
    for name, v in laid.items():
        v = np.ascontiguousarray(v)
        arrays["in_" + name] = v
        args.append(nc.dram_tensor("in_" + name, v.shape, mybir.dt.from_np(v.dtype), kind="ExternalInput").ap())
    res = nc.dram_tensor("out_0", a["x"].shape, mybir.dt.float32, kind="ExternalOutput").ap()
    gnn_moe_layer(nc, *args, res)
    r = run_bass_kernel_spmd(nc, [arrays], core_ids=[0])
    return r.results[0]["out_0"]
```

```python
import numpy as np
import concourse.bass as bass
from concourse import mybir
from contextlib import ExitStack

P = 128
IW = 512
CK = 4
WS = 128.0
ROW = 132
TS = 256


def gnn_moe_layer(nc, x, adj_tiles, adj_rows, w_proj, b_proj, w_gcn, b_gcn,
                  w_gate, b_gate, w1, b1, w2, b2, out):
    fp32, bf16, fp16, i32 = mybir.dt.float32, mybir.dt.bfloat16, mybir.dt.float16, mybir.dt.int32
    ALU, ACT, AX = mybir.AluOpType, mybir.ActivationFunctionType, mybir.AxisListType

    N, D = x.shape
    C = N // P
    TOPK = 350
    EPS = 1e-5
    E, H = b2.shape[0], w1.shape[2]
    HB = H // P
    NB = N // IW
    NK = C // CK
    NBUF = 4
    R = 4
    SEG = P // R
    STEPS = 15
    SUB = IW // P
    Q = 2 * SUB
    RS = N + TS
    NT = 2 * N // TS + E
    NX = 8
    AHEAD = 2
    NOWHERE = 1 << 20

    xs = nc.dram_tensor("routed_rows", (E * RS + TS, ROW), fp32).ap()
    ys = nc.dram_tensor("expert_rows", (2 * N, D), fp32).ap()

    ctx = ExitStack()
    with ctx:
        ctx.enter_context(nc.allow_low_precision(reason="counts of at most 128 are exact"))

        def sb(name, shape, dt=fp32):
            return ctx.enter_context(nc.sbuf_tensor(name, shape, dt))

        def sem(name):
            return ctx.enter_context(nc.semaphore(name))

        xres = sb("xres", [P, C, D])
        g_sb = sb("g_sb", [P, C, D])
        feat_t = sb("feat_t", [P, N])
        w1h, w1l = sb("w1h", [P, E, H], fp16), sb("w1l", [P, E, H], fp16)
        w2h, w2l = sb("w2h", [P, E, HB, D], fp16), sb("w2l", [P, E, HB, D], fp16)
        wstage = sb("wstage", [P, E * H])
        abuf = sb("abuf", [P, NBUF, CK, IW])
        tbuf = sb("tbuf", [P, NBUF, CK, IW])
        ind = sb("ind", [P, NBUF, CK, IW], bf16)
        aug = sb("aug", [P, 2, 2, SUB, ROW])
        xnt = wstage[:, 0:IW]

        t_flat = tbuf[:, :, :, :].rearrange("p a b c -> p (a b c)")
        xnorm = t_flat[:, 0:N].rearrange("p (c d) -> p c d", d=D)
        xnorm_t = t_flat[:, N:2 * N]
        h2t = ind[:, :, :, :].rearrange("p a b c -> p (a b c)").bitcast(fp32)[:, 0:2 * IW].rearrange(
            "p (a i) -> p a i", a=2)
        a_flat = abuf[:, :, :, :].rearrange("p a b c -> p (a b c)")
        xld = a_flat[:, 0:NX * 2 * ROW].rearrange("p (n s w) -> p n s w", n=NX, s=2)
        ysb = a_flat[:, 2560:2560 + NX * TS].rearrange("p (n s d) -> p n s d", n=NX, s=2)
        yin = a_flat[:, 5120:5120 + 4 * IW].rearrange("p (q k c d) -> p q k c d", q=2, k=2, d=D)
        relu = t_flat[:, 0:2 * HB * TS].rearrange("p (q h s) -> p q h s", q=2, h=HB)
        t_half = t_flat[:, 2 * HB * TS:].bitcast(fp16)
        hh = t_half[:, 0:2 * HB * TS].rearrange("p (q h s) -> p q h s", q=2, h=HB)
        hl = t_half[:, 2 * HB * TS:4 * HB * TS].rearrange("p (q h s) -> p q h s", q=2, h=HB)
        xh = t_half[:, 4 * HB * TS:4 * HB * TS + 2 * TS].rearrange("p (q s) -> p q s", q=2)
        xl = t_half[:, 4 * HB * TS + 2 * TS:4 * HB * TS + 4 * TS].rearrange("p (q s) -> p q s", q=2)

        ident = sb("ident", [P, P])
        ones_f = sb("ones_f", [P, P])
        ones_bf = sb("ones_bf", [P, P], bf16)
        before = sb("before", [P, P], bf16)
        same_row = sb("same_row", [P, P], bf16)
        before_row = sb("before_row", [P, P], bf16)
        ones_h = sb("ones_h", [2, P], fp16)
        wp_sb = sb("wp_sb", [P, D])
        wg_sb = sb("wg_sb", [P, D])
        bp_sb = sb("bp_sb", [P, 1])
        bg_sb = sb("bg_sb", [P, 1])
        gate_w = sb("gate_w", [P, E])
        gate_b = sb("gate_b", [1, E])
        b1_sb = sb("b1_sb", [P, E * HB])
        b2_f = sb("b2_f", [2, E, D])
        b2_h = sb("b2_h", [2, E, D], fp16)
        b2_hl = sb("b2_hl", [2, E, D], fp16)
        pidx = sb("pidx", [P, 1], i32)
        is_p1 = sb("is_p1", [2, 1])
        is_p0 = sb("is_p0", [2, 1])
        stats = sb("stats", [P, C, 6])
        mean = sb("mean", [P, C])
        var = sb("var", [P, C])
        rstd = sb("rstd", [P, C])
        tmp = sb("tmp", [P, C])
        rowid = sb("rowid", [P, C], i32)
        rowidf = sb("rowidf", [P, C])
        count = sb("count", [P, C])
        key = sb("key", [P, C])
        keyrow = xnorm[0:1, :, :].rearrange("o c d -> o (c d)")
        keyflag = xnorm_t[0:1, :]
        nflag = sb("nflag", [1, 1])
        nrounds = sb("nrounds", [1, 1], i32)
        top = sb("top", [1, 8])
        ids = sb("ids", [1, 8], i32)
        rowval = sb("rowval", [P, P])
        rowsc = sb("rowsc", [P, P])
        rowbf = wstage[:, IW:IW + 2 * P].bitcast(bf16).rearrange("p (k f) -> p k f", k=4)
        rowgt = sb("rowgt", [P, P])
        roweq = sb("roweq", [P, P])
        row_t = sb("row_t", [P, P])
        bits = sb("bits", [P, STEPS, 4], i32)
        thr = sb("thr", [P, 1])
        cand = sb("cand", [P, 4], i32)
        ncand = sb("ncand", [P, 4], bf16)
        okc = sb("okc", [P, 4])
        pair = sb("pair", [P, 2], bf16)
        need = sb("need", [P, 1])
        fixed = sb("fixed", [P, R])
        scores = sb("scores", [P, SUB, E])
        masked = sb("masked", [P, SUB, E])
        hit = sb("hit", [P, SUB, E])
        oh = sb("oh", [P, Q, E], bf16)
        eidx = sb("eidx", [P, SUB, E])
        eidx_i = sb("eidx_i", [P, SUB, E], i32)
        m1 = sb("m1", [P, SUB])
        m2 = sb("m2", [P, SUB])
        pick = sb("pick", [P, SUB])
        ex = sb("ex", [P, SUB])
        p1 = sb("p1", [P, SUB])
        dest = sb("dest", [P, 2, C], i32)
        place = sb("place", [P, Q, E])
        slots = sb("slots", [P, 2, Q], i32)
        base = sb("base", [P, E])
        base_i = sb("base_i", [P, E], i32)
        pad = sb("pad", [P, 2, ROW])
        tnum_i = sb("tnum_i", [1, NT + AHEAD, E], i32)
        tnum = sb("tnum", [1, NT + AHEAD, E])
        table = wstage[0:1, IW:].rearrange("o (k t e) -> o k t e", e=E, t=(E * H - IW) // E // 2)
        past = table[:, 0, 0:NT + AHEAD, :]
        jump = table[:, 1, 0:NT + AHEAD, :]
        tiles = sb("tiles", [1, E])
        tiles_i = sb("tiles_i", [1, E], i32)
        ends = sb("ends", [1, E])
        skip = sb("skip", [1, E])
        tile_e = sb("tile_e", [1, NT + AHEAD])
        tile_ei = sb("tile_ei", [1, NT + AHEAD], i32)
        tile_r = sb("tile_r", [1, NT + AHEAD])
        tile_ri = sb("tile_ri", [1, NT + AHEAD], i32)
        pad_i = sb("pad_i", [1, E], i32)

        bank = [ctx.enter_context(nc.psum_tensor(f"bank{i}", [P, 512], fp32)) for i in range(8)]
        ps_feat, ps_cnt = bank[0:2], bank[2:4]
        ps_x2, ps_xn = bank[4], bank[5]
        ps_gate = bank[6][:, 0:SUB * E]
        ps_ncand = bank[6][:, 64:68]
        ps_tie = bank[6][:, 72:74]
        ps_place = bank[7][:, 0:Q * E].rearrange("p (q e) -> p q e", e=E)
        ps_total = bank[7][:, Q * E:Q * E + E]
        ps_rowt = bank[7][:, 128:256]
        ps_fix = bank[7][:, 256:256 + R]

        s_x = sem("s_x")
        s_w = sem("s_w")
        s_small = sem("s_small")
        s_w1 = sem("s_w1")
        s_w2 = sem("s_w2")
        s_split = sem("s_split")
        s_const = sem("s_const")
        s_ident = sem("s_ident")
        s_pool = sem("s_pool")
        s_dve = sem("s_dve")
        s_xn1 = sem("s_xn1")
        s_tr = sem("s_tr")
        s_trc = sem("s_trc")
        s_proj = sem("s_proj")
        s_h2 = sem("s_h2")
        s_gp = sem("s_gp")
        s_g = sem("s_g")
        s_a = [sem(f"s_a{i}") for i in range(NBUF)]
        s_sq = sem("s_sq")
        s_t = sem("s_t")
        s_ind = sem("s_ind")
        s_pe = sem("s_pe")
        s_ev = sem("s_ev")
        s_cnt = sem("s_cnt")
        s_key = sem("s_key")
        s_keyrow = sem("s_keyrow")
        s_nr = sem("s_nr")
        s_ids = sem("s_ids")
        s_rows = sem("s_rows")
        s_fdve = sem("s_fdve")
        s_rsq = sem("s_rsq")
        s_val = sem("s_val")
        s_part = sem("s_part")
        s_tot = sem("s_tot")
        s_keep = sem("s_keep")
        s_rt = sem("s_rt")
        s_rtc = sem("s_rtc")
        s_fmm = sem("s_fmm")
        s_fix = sem("s_fix")
        s_fixed = sem("s_fixed")
        s_spare = sem("s_spare")
        s_r1 = sem("s_r1")
        s_x2 = sem("s_x2")
        s_xn = sem("s_xn")
        s_r2 = sem("s_r2")
        s_xt = sem("s_xt")
        s_ax = sem("s_ax")
        s_r3 = sem("s_r3")
        s_gc = sem("s_gc")
        s_df = sem("s_df")
        s_ex = sem("s_ex")
        s_oh = sem("s_oh")
        s_meta = sem("s_meta")
        s_r4 = sem("s_r4")
        s_sl = sem("s_sl")
        s_scat = [sem(f"s_scat{i}") for i in range(2)]
        s_padb = sem("s_padb")
        s_padd = sem("s_padd")
        s_padr = sem("s_padr")
        s_tab = sem("s_tab")
        s_pads = sem("s_pads")
        s_xl = [sem(f"s_xl{i}") for i in range(NX)]
        s_xp = sem("s_xp")
        s_xh = sem("s_xh")
        s_xlo = sem("s_xlo")
        s_h = sem("s_h")
        s_relu = sem("s_relu")
        s_hs = sem("s_hs")
        s_y = sem("s_y")
        s_yo = sem("s_yo")
        s_sc = [sem(f"s_sc{i}") for i in range(NX)]
        s_yl = [sem(f"s_yl{i}") for i in range(2)]
        s_sum = sem("s_sum")
        s_out = sem("s_out")

        block = ctx.enter_context(nc.Block())

        @block.sync
        def _(sp):
            sp.dma_start(xres[:, :, :], x.rearrange("(c p) d -> p c d", p=P)).then_inc(s_x, 16)
            sp.dma_start(wstage[:, :], w1.rearrange("p e h -> p (e h)")).then_inc(s_w1, 16)

            def load_block(ib, first=False):
                for k in range(NK):
                    if not (first and k < NBUF):
                        sp.wait_ge(s_t, ib * NK + k - NBUF + 1)
                    sp.dma_start(abuf[:, k % NBUF, :, :], adj_tiles[bass.ds(ib, 1), k, :, :, :]
                                 .rearrange("o p c i -> p (o c) i")).then_inc(s_a[k % NBUF], 16)

            load_block(0, first=True)
            sp.wait_ge(s_split, 1)
            sp.dma_start(wstage[:, :], w2.rearrange("p e b d -> p (e b d)")).then_inc(s_w2, 16)
            sp.wait_ge(s_padb, 1)
            sp.dma_start(xs[E * RS:E * RS + TS, :].rearrange("(s p) w -> p s w", p=P), pad[:, :, :]
                         ).then_inc(s_padd, 16)
            with sp.Fori(1, NB) as ib:
                load_block(ib)

            sp.wait_ge(s_key, 1)
            sp.dma_start(keyrow.rearrange("o (p t) -> o p t", p=P), key[:, :].rearrange("p (o t) -> p o t", o=1)
                         ).then_inc(s_keyrow, 16)
            sp.wait_ge(s_nr, 1)
            rounds = sp.value_load(nrounds[0:1, 0:1], min_val=1, max_val=N // R)
            with sp.Fori(0, rounds) as r:
                sp.wait_ge(s_ids, r + 1)
                sp.sem_inc(s_spare, 1)
                for q in range(R):
                    row = sp.value_load(ids[0:1, q:q + 1], min_val=0, max_val=N - 1)
                    sp.dma_start(rowval[q * SEG:(q + 1) * SEG, :], adj_rows[bass.ds(row, 1), :]
                                 .rearrange("o (s f) -> s (o f)", s=SEG)).then_inc(s_rows, 16)

            sp.wait_ge(s_padr, 1)
            for e in range(E):
                row = sp.value_load(pad_i[0:1, e:e + 1], min_val=0, max_val=E * RS - TS)
                sp.dma_start(xs[bass.ds(row, TS), :].rearrange("(s p) w -> p s w", p=P), pad[:, :, :]
                             ).then_inc(s_pads, 16)
            sp.wait_ge(s_pads, 16 * E)
            sp.wait_ge(s_padd, 16)
            for i in range(2):
                sp.wait_ge(s_scat[i], NB // 2 * Q * 16)
            sp.wait_ge(s_tab, 1)

            def load_tile(t, u, first=False):
                if not first:
                    sp.wait_ge(s_sc[u], (t - u) // NX * 32)
                    sp.sem_inc(s_spare, 1)
                row = sp.value_load(tile_ri[0:1, bass.ds(t, 1)], min_val=0, max_val=E * RS)
                sp.dma_start(xld[:, u, :, :], xs[bass.ds(row, TS), :].rearrange("(s p) w -> p s w", p=P)
                             ).then_inc(s_xl[u], 16)

            for u in range(NX):
                load_tile(u, u, first=True)
            with sp.Fori(1, NT // NX) as g:
                for u in range(NX):
                    sp.wait_ge(s_sc[u], g * 32)
                    sp.sem_inc(s_spare, 1)
                    row = sp.value_load(tile_ri[0:1, bass.ds(g * NX + u, 1)], min_val=0, max_val=E * RS)
                    sp.dma_start(xld[:, u, :, :], xs[bass.ds(row, TS), :].rearrange("(s p) w -> p s w", p=P)
                                 ).then_inc(s_xl[u], 16)
            for u in range(AHEAD):
                sp.wait_ge(s_sc[u], NT // NX * 32)
                row = sp.value_load(tile_ri[0:1, NT + u:NT + u + 1], min_val=0, max_val=E * RS)
                sp.dma_start(xld[:, u, :, :], xs[bass.ds(row, TS), :].rearrange("(s p) w -> p s w", p=P)
                             ).then_inc(s_xl[u], 16)

            for u in range(NX):
                sp.wait_ge(s_sc[u], NT // NX * 32)
            for g in range(NK):
                if g >= 2:
                    sp.wait_ge(s_sum, g - 1)
                for k in range(2):
                    sp.dma_start(yin[:, g % 2, k, :, :],
                                 ys[k * N + g * IW:k * N + (g + 1) * IW, :].rearrange("(c p) d -> p c d", p=P)
                                 ).then_inc(s_yl[g % 2], 16)
            sp.wait_ge(s_out, NK * 16)

        @block.gpsimd
        def _(pool):
            links = [0]

            def link(ins):
                links[0] += 1
                ins.then_inc(s_pool, 1)
                pool.wait_ge(s_pool, links[0])

            pool.dma_start(wp_sb[:, :], w_proj).then_inc(s_w, 16)
            pool.dma_start(wg_sb[:, :], w_gcn).then_inc(s_w, 16)
            pool.dma_start(bp_sb[:, :], b_proj.rearrange("(p o) -> p o", o=1)).then_inc(s_w, 16)
            pool.dma_start(bg_sb[:, :], b_gcn.rearrange("(p o) -> p o", o=1)).then_inc(s_w, 16)
            pool.dma_start(b1_sb[:, :], b1).then_inc(s_small, 16)
            pool.dma_start(gate_w[:, :], w_gate).then_inc(s_small, 16)
            pool.dma_start(gate_b[:, :], b_gate.rearrange("(o e) -> o e", o=1)).then_inc(s_small, 16)
            for i in range(2):
                pool.dma_start(b2_f[i:i + 1, :, :], b2.rearrange("(o e) d -> o e d", o=1)).then_inc(s_small, 16)
            link(pool.memset(ident[:, :], 0.0))
            pool.affine_select(out=ident[:, :], in_=ident[:, :], compare_op=ALU.not_equal, fill=1.0, base=0,
                               pattern=[[-1, P]], channel_multiplier=1).then_inc(s_ident, 1)
            pool.memset(ones_bf[:, :], 1.0)
            pool.memset(ones_f[:, :], 1.0)
            link(pool.memset(ones_h[:, :], 1.0))
            link(pool.affine_select(out=before[:, :], in_=ones_bf[:, :], compare_op=ALU.is_ge, fill=0.0, base=-1,
                                    pattern=[[1, P]], channel_multiplier=-1))
            grid = [[-SEG, R], [0, SEG]]
            link(pool.affine_select(out=same_row[:, :].rearrange("p (r s) -> p r s", r=R),
                                    in_=ones_bf[:, :].rearrange("p (r s) -> p r s", r=R),
                                    compare_op=ALU.is_ge, fill=0.0, base=0, pattern=grid, channel_multiplier=1))
            link(pool.affine_select(out=same_row[:, :].rearrange("p (r s) -> p r s", r=R),
                                    in_=same_row[:, :].rearrange("p (r s) -> p r s", r=R),
                                    compare_op=ALU.is_ge, fill=0.0, base=SEG - 1, pattern=[[SEG, R], [0, SEG]],
                                    channel_multiplier=-1))
            link(pool.tensor_tensor(before_row[:, :], before[:, :], same_row[:, :], ALU.mult))
            pool.iota(rowid[:, :], [[P, C]], base=1, channel_multiplier=1)
            pool.iota(dest[:, :, :], [[N, 2], [P, C]], base=0, channel_multiplier=1)
            pool.iota(eidx_i[:, :, :], [[0, SUB], [-1, E]], base=E, channel_multiplier=0)
            pool.iota(base_i[:, :], [[RS, E]], base=0, channel_multiplier=0)
            pool.iota(tnum_i[:, :, :], [[1, NT + AHEAD], [0, E]], base=0, channel_multiplier=0)
            link(pool.iota(pidx[:, :], [[0, 1]], base=0, channel_multiplier=1))
            for b in range(STEPS):
                for k in range(4):
                    pool.memset(bits[:, b, k:k + 1], k << (2 * (STEPS - 1 - b)))
            pool.memset(aug[:, :, :, :, :], 0.0)
            pool.memset(pad[:, :, :], 0.0)
            link(pool.memset(ncand[:, :], float(P)))
            pool.memset(pad[:, :, D:D + 1].bitcast(i32), NOWHERE).then_inc(s_padb, 1)
            pool.wait_ge(s_padb, 1)
            pool.tensor_copy(eidx[:, :, :], eidx_i[:, :, :])
            pool.tensor_copy(rowidf[:, :], rowid[:, :])
            pool.tensor_copy(base[:, :], base_i[:, :])
            pool.tensor_copy(tnum[:, :, :], tnum_i[:, :, :])
            link(pool.tensor_copy(is_p1[:, :], pidx[0:2, :]))
            link(pool.tensor_scalar(is_p0[:, :], is_p1[:, :], -1.0, 1.0, ALU.mult, ALU.add))
            pool.wait_ge(s_small, 80)
            link(pool.tensor_scalar(b2_f[:, :, :], b2_f[:, :, :], WS, 0.0, ALU.mult, ALU.add))
            link(pool.tensor_copy(b2_h[:, :, :], b2_f[:, :, :]))
            link(pool.tensor_tensor(b2_f[:, :, :], b2_f[:, :, :], b2_h[:, :, :], ALU.subtract))
            link(pool.tensor_scalar(b2_f[:, :, :], b2_f[:, :, :], is_p1[:, 0:1], 0.0, ALU.mult, ALU.add))
            link(pool.tensor_scalar(b2_hl[:, :, :], b2_h[:, :, :], is_p0[:, 0:1], 0.0, ALU.mult, ALU.add))
            pool.tensor_tensor(b2_hl[:, :, :], b2_hl[:, :, :], b2_f[:, :, :], ALU.add).then_inc(s_const, 1)

            for s_in, hi, lo in ((s_w1, w1h[:, :, :].rearrange("p e h -> p (e h)"), w1l[:, :, :].rearrange("p e h -> p (e h)")),
                                 (s_w2, w2h[:, :, :, :].rearrange("p e b d -> p (e b d)"),
                                  w2l[:, :, :, :].rearrange("p e b d -> p (e b d)"))):
                pool.wait_ge(s_in, 16)
                link(pool.tensor_scalar(wstage[:, :], wstage[:, :], WS, 0.0, ALU.mult, ALU.add))
                link(pool.tensor_copy(hi, wstage[:, :]))
                pool.tensor_tensor(lo, wstage[:, :], hi, ALU.subtract).then_inc(s_split, 1)

            for b in range(NB):
                pool.wait_ge(s_sl, b + 1)
                pool.wait_ge(s_meta, b + 1)
                pool.wait_ge(s_ax, b + 1)
                for k in range(2):
                    for cc in range(SUB):
                        pool.indirect_dma_start(
                            xs, bass.IndirectOffsetOnAxis(ap=slots[:, b % 2, k * SUB + cc:k * SUB + cc + 1], axis=0),
                            aug[:, b % 2, k, cc, :], None).then_inc(s_scat[b % 2], 16)

            def store_tile(t, u, loop=True):
                pool.wait_ge(s_yo, t + 1)
                if loop:
                    pool.sem_inc(s_spare, 1)
                for s in range(2):
                    pool.indirect_dma_start(
                        ys, bass.IndirectOffsetOnAxis(ap=xld[:, u, s, D:D + 1].bitcast(i32), axis=0),
                        ysb[:, u, s, :], None, bounds_check=2 * N - 1, oob_is_err=False).then_inc(s_sc[u], 16)

            with pool.Fori(0, NT // NX) as g:
                for u in range(NX):
                    store_tile(g * NX + u, u)

        @block.vector
        def _(dve):
            chain = [0]

            def link(ins):
                chain[0] += 1
                ins.then_inc(s_dve, 1)
                dve.wait_ge(s_dve, chain[0])

            def norm_scale(c0, n):
                st, mn, vr, rs, tp = (a[:, c0:c0 + n] for a in (stats, mean, var, rstd, tmp))
                link(dve.tensor_tensor(mn, st[:, :, 1], st[:, :, 4], ALU.add))
                link(dve.tensor_tensor(tp, st[:, :, 1], st[:, :, 4], ALU.subtract))
                link(dve.tensor_tensor(vr, st[:, :, 2], st[:, :, 5], ALU.add))
                link(dve.tensor_tensor(tp, tp, tp, ALU.mult))
                link(dve.tensor_scalar(mn, mn, 0.5, None, ALU.mult))
                link(dve.tensor_scalar(tp, tp, 0.25, EPS, ALU.mult, ALU.add))
                link(dve.scalar_tensor_tensor(vr, vr, 1.0 / D, tp, ALU.mult, ALU.add))
                link(dve.tensor_scalar(tp.bitcast(i32), vr.bitcast(i32), 1, None, ALU.logical_shift_right))
                link(dve.tensor_scalar(rs.bitcast(i32), tp.bitcast(i32), -1.0, float(0x5F3759DF), ALU.mult, ALU.add))
                for _ in range(4):
                    link(dve.tensor_tensor(tp, rs, rs, ALU.mult))
                    link(dve.tensor_tensor(tp, tp, vr, ALU.mult))
                    link(dve.tensor_scalar(tp, tp, -0.5, 1.5, ALU.mult, ALU.add))
                    link(dve.tensor_tensor(rs, rs, tp, ALU.mult))

            dve.wait_ge(s_x, 16)
            for c in range(C):
                last = dve.bn_stats(stats[:, c, :], xres[:, c, :])
            link(last)
            norm_scale(0, C)
            for c in range(C):
                ins = dve.tensor_scalar(xnorm[:, c, :], xres[:, c, :], mean[:, c:c + 1], rstd[:, c:c + 1],
                                        ALU.subtract, ALU.mult)
                if c % CK == CK - 1:
                    ins.then_inc(s_xn1, 1)
            for g in range(NK):
                dve.wait_ge(s_tr, g + 1)
                dve.tensor_copy(xnorm_t[:, g * IW:(g + 1) * IW], [ps_x2, ps_xn][g % 2][:, :]).then_inc(s_trc, 1)
                if g:
                    dve.wait_ge(s_gp, g)
                    dve.tensor_copy(g_sb[:, (g - 1) * CK:g * CK, :],
                                    ps_feat[(g - 1) % 2][:, :].rearrange("p (c d) -> p c d", c=CK)).then_inc(s_g, 1)
            dve.wait_ge(s_gp, NK)
            dve.tensor_copy(g_sb[:, (NK - 1) * CK:, :],
                            ps_feat[(NK - 1) % 2][:, :].rearrange("p (c d) -> p c d", c=CK)).then_inc(s_g, 1)

            def square_blocks(pb, first=False):
                for m in range(2 * NK):
                    n = pb * 2 * NK + m
                    b = m % NBUF
                    dve.wait_ge(s_a[b], (pb * (2 * NK // NBUF) + m // NBUF + 1) * 16)
                    dve.scalar_tensor_tensor(abuf[:, b, :, :], abuf[:, b, :, :], 0.0, abuf[:, b, :, :],
                                             ALU.max, ALU.mult).then_inc(s_sq, 1)
                    if not (first and m == 0):
                        indicate(n - 1, (m - 1) % NBUF, first and m <= NBUF)
                    if m % NK == 1 and not (first and m == 1):
                        counts_out(pb * 2 + m // NK - 1, (m // NK - 1) % 2)

            def indicate(n, b, fresh):
                dve.wait_ge(s_t, n + 1)
                if not fresh:
                    dve.wait_ge(s_pe, n - NBUF + 1)
                dve.tensor_scalar(ind[:, b, :, :], tbuf[:, b, :, :], 0.0, None, ALU.is_gt).then_inc(s_ind, 1)

            def counts_out(ib, parity):
                dve.wait_ge(s_pe, (ib + 1) * NK)
                dve.tensor_copy(count[:, bass.ds(ib * SUB, SUB)], ps_cnt[parity][:, 0:SUB]).then_inc(s_cnt, 1)

            square_blocks(0, first=True)
            with dve.Fori(1, NB // 2) as pb:
                square_blocks(pb)
            indicate(NB * NK - 1, NBUF - 1, False)
            counts_out(NB - 1, 1)
            dve.wait_ge(s_cnt, NB)

            dve.wait_ge(s_const, 1)
            dve.wait_ge(s_split, 2)
            link(dve.tensor_scalar(key[:, :], count[:, :], float(TOPK), None, ALU.is_gt))
            dve.tensor_tensor(key[:, :], key[:, :], rowidf[:, :], ALU.mult).then_inc(s_key, 1)
            dve.wait_ge(s_keyrow, 16)
            link(dve.tensor_scalar(keyflag, keyrow, 0.0, None, ALU.is_gt))
            link(dve.tensor_reduce(nflag[:, :], keyflag, AX.X, ALU.add))
            link(dve.tensor_scalar(nflag[:, :], nflag[:, :], 1.0 / R, 0.5 - 0.5 / R, ALU.mult, ALU.add))
            dve.tensor_scalar(nrounds[:, :], nflag[:, :], 1.0, None, ALU.max).then_inc(s_nr, 1)
            dve.wait_ge(s_nr, 1)
            rounds = dve.value_load(nrounds[0:1, 0:1], min_val=1, max_val=N // R)
            CHAIN = 2 + 3 * STEPS + 1 + 4 + R
            TOTS = STEPS + 1

            with dve.Fori(0, rounds) as r:
                links = [0]

                def rlink(ins):
                    links[0] += 1
                    ins.then_inc(s_fdve, 1)
                    dve.wait_ge(s_fdve, r * CHAIN + links[0])

                rlink(dve.max(top[:, :], keyrow))
                dve.tensor_scalar(ids[:, :], top[:, :], -1.0, 0.0, ALU.add, ALU.max).then_inc(s_ids, 1)
                dve.scalar_tensor_tensor(keyrow, keyrow, top[:, R - 1:R], keyrow, ALU.is_lt, ALU.mult)
                rlink(dve.memset(thr[:, :], 0.0))
                dve.wait_ge(s_rows, (r + 1) * 16 * R)
                dve.scalar_tensor_tensor(rowval[:, :], rowval[:, :], 0.0, rowval[:, :], ALU.max, ALU.mult
                                         ).then_inc(s_rsq, 1)
                dve.wait_ge(s_val, r + 1)
                for b in range(STEPS):
                    rlink(dve.tensor_tensor(cand[:, :], bits[:, b, :], thr[:, :].bitcast(i32).to_broadcast([P, 4]),
                                            ALU.bitwise_or))
                    for k in range(1, 4):
                        last = dve.tensor_scalar(rowbf[:, k, :], rowval[:, :], cand[:, k:k + 1].bitcast(fp32), None,
                                                 ALU.is_ge, ALU.add, accum_out=ncand[:, k:k + 1])
                    last.then_inc(s_part, 1)
                    dve.wait_ge(s_tot, r * TOTS + b + 1)
                    rlink(dve.scalar_tensor_tensor(okc[:, :], ps_ncand, float(TOPK), cand[:, :].bitcast(fp32),
                                                   ALU.is_ge, ALU.mult))
                    rlink(dve.tensor_reduce(thr[:, :], okc[:, :], AX.X, ALU.max))
                dve.tensor_scalar(rowgt[:, :], rowval[:, :], thr[:, 0:1], None, ALU.is_gt, ALU.add,
                                  accum_out=pair[:, 0:1])
                dve.tensor_scalar(roweq[:, :], rowval[:, :], thr[:, 0:1], None, ALU.is_equal, ALU.add,
                                  accum_out=pair[:, 1:2]).then_inc(s_part, 1)
                dve.wait_ge(s_part, (r + 1) * TOTS)
                rlink(dve.tensor_tensor_scan(rowsc[:, :], ones_f[:, :], roweq[:, :], 0.0, ALU.mult, ALU.add))
                dve.wait_ge(s_tot, (r + 1) * TOTS)
                rlink(dve.tensor_scalar(need[:, :], ps_tie[:, 0:1], -1.0, float(TOPK), ALU.mult, ALU.add))
                rlink(dve.tensor_tensor(need[:, :], need[:, :], ps_tie[:, 1:2], ALU.subtract))
                rlink(dve.scalar_tensor_tensor(roweq[:, :], rowsc[:, :], need[:, 0:1], roweq[:, :],
                                               ALU.is_le, ALU.mult))
                rlink(dve.tensor_tensor(rowgt[:, :], rowgt[:, :], roweq[:, :], ALU.add))
                dve.tensor_tensor(rowgt[:, :], rowgt[:, :], rowval[:, :], ALU.mult).then_inc(s_keep, 1)
                dve.wait_ge(s_rt, r + 1)
                dve.tensor_copy(row_t[:, :], ps_rowt).then_inc(s_rtc, 1)
                dve.wait_ge(s_fix, r + 1)
                dve.sem_inc(s_spare, 1)
                rows = [dve.value_load(ids[0:1, q:q + 1], min_val=0, max_val=N - 1) for q in range(R)]
                for q in range(R):
                    rlink(dve.tensor_copy(feat_t[:, bass.ds(rows[q], 1)], fixed[:, q:q + 1]))
                assert links[0] == CHAIN, links
            dve.memset(tmp[:, :], 0.0).then_inc(s_fixed, 1)

            def spread(v):
                return v[:, :].rearrange("p (c o) -> p c o", o=1).to_broadcast([P, SUB, E])

            def first_of_max(src, m, onehot):
                link(dve.tensor_reduce(m[:, :], src, AX.X, ALU.max))
                link(dve.tensor_tensor(hit[:, :, :], src, spread(m), ALU.is_equal))
                link(dve.tensor_tensor(hit[:, :, :], hit[:, :, :], eidx[:, :, :], ALU.mult))
                link(dve.tensor_reduce(pick[:, :], hit[:, :, :], AX.X, ALU.max))
                return dve.tensor_tensor(onehot, eidx[:, :, :], spread(pick), ALU.is_equal)

            def normalise(b):
                q = b % 2
                dve.wait_ge(s_r1, b + 1)
                xb = xres[:, b * SUB:(b + 1) * SUB, :]
                dve.tensor_tensor(xb, xb, ps_x2[:, :].rearrange("p (c d) -> p c d", c=SUB), ALU.add
                                  ).then_inc(s_x2, 1)
                dve.wait_ge(s_x2, b + 1)
                for cc in range(SUB):
                    last = dve.bn_stats(stats[:, b * SUB + cc, :], xres[:, b * SUB + cc, :])
                link(last)
                norm_scale(b * SUB, SUB)
                if b >= 2:
                    dve.wait_ge(s_scat[q], b // 2 * Q * 16)
                for cc in range(SUB):
                    c = b * SUB + cc
                    last = dve.tensor_scalar(aug[:, q, 0, cc, 0:D], xres[:, c, :], mean[:, c:c + 1],
                                             rstd[:, c:c + 1], ALU.subtract, ALU.mult)
                last.then_inc(s_xn, 1)

            def choose(b):
                q = b % 2
                dve.wait_ge(s_r3, b + 1)
                dve.tensor_copy(scores[:, :, :], ps_gate.rearrange("p (c e) -> p c e", e=E)).then_inc(s_gc, 1)
                dve.wait_ge(s_gc, b + 1)
                if b:
                    dve.wait_ge(s_r4, b)
                link(first_of_max(scores[:, :, :], m1, oh[:, 0:SUB, :]))
                link(dve.scalar_tensor_tensor(masked[:, :, :], oh[:, 0:SUB, :], -3.0e38, scores[:, :, :],
                                              ALU.mult, ALU.add))
                first_of_max(masked[:, :, :], m2, oh[:, SUB:Q, :]).then_inc(s_oh, 1)
                dve.tensor_tensor(ex[:, :], m2[:, :], m1[:, :], ALU.subtract).then_inc(s_df, 1)
                for k in range(2):
                    dve.tensor_copy(aug[:, q, k, :, D].bitcast(i32), dest[:, k, b * SUB:(b + 1) * SUB])
                dve.wait_ge(s_ex, b + 1)
                link(dve.tensor_scalar(p1[:, :], ex[:, :], 1.0, None, ALU.add))
                link(dve.reciprocal(p1[:, :], p1[:, :]))
                link(dve.tensor_scalar(p1[:, :], p1[:, :], 1.0 / WS, None, ALU.mult))
                dve.tensor_copy(aug[:, q, 0, :, D + 1], p1[:, :])
                dve.tensor_tensor(aug[:, q, 1, :, D + 1], ex[:, :], p1[:, :], ALU.mult).then_inc(s_meta, 1)

            def assign(b):
                q = b % 2
                dve.wait_ge(s_r4, b + 1)
                link(dve.tensor_tensor(place[:, :, :], ps_place,
                                       base[:, :].rearrange("p (o e) -> p o e", o=1).to_broadcast([P, Q, E]), ALU.add))
                link(dve.tensor_tensor(place[:, :, :], place[:, :, :], oh[:, :, :], ALU.mult))
                if b >= 2:
                    dve.wait_ge(s_scat[q], b // 2 * Q * 16)
                dve.tensor_reduce(slots[:, q, :], place[:, :, :], AX.X, ALU.add)
                dve.tensor_tensor(base[:, :], base[:, :], ps_total, ALU.add).then_inc(s_sl, 1)
                dve.wait_ge(s_sl, b + 1)

            for b in range(NB):
                normalise(b)
                if b:
                    choose(b - 1)
                    assign(b - 1)
            choose(NB - 1)
            assign(NB - 1)

            dve.tensor_copy(pad_i[:, :], base[0:1, :]).then_inc(s_padr, 1)
            first = dve.tensor_tensor(tiles[:, :], base[0:1, :], base_i[0:1, :], ALU.subtract)
            link(first)
            link(dve.tensor_scalar(tiles_i[:, :], tiles[:, :], 1.0 / TS, 0.5 - 0.5 / TS, ALU.mult, ALU.add))
            link(dve.tensor_copy(tiles[:, :], tiles_i[:, :]))
            link(dve.tensor_tensor_scan(ends[:, :], ones_f[0:1, 0:E], tiles[:, :], 0.0, ALU.mult, ALU.add))
            dve.wait_ge(s_split, 2)
            link(dve.tensor_scalar(skip[:, :], tiles[:, :], -float(TS), float(RS), ALU.mult, ALU.add))
            TT = [1, NT + AHEAD, E]
            link(dve.tensor_tensor(past, tnum[:, :, :],
                                   ends[:, :].rearrange("p (o e) -> p o e", o=1).to_broadcast(TT), ALU.is_ge))
            link(dve.tensor_reduce(tile_e[:, :], past, AX.X, ALU.add))
            link(dve.tensor_tensor(jump, past,
                                   skip[:, :].rearrange("p (o e) -> p o e", o=1).to_broadcast(TT), ALU.mult))
            link(dve.tensor_reduce(tile_r[:, :], jump, AX.X, ALU.add))
            link(dve.scalar_tensor_tensor(tile_r[:, :], tnum[:, :, 0], float(TS), tile_r[:, :], ALU.mult, ALU.add))
            dve.tensor_scalar(tile_ei[:, :], tile_e[:, :], float(E - 1), None, ALU.min)
            dve.tensor_scalar(tile_ri[:, :], tile_r[:, :], float(E * RS), None, ALU.min).then_inc(s_tab, 1)

            def cut_x(t, q, fresh=False):
                dve.wait_ge(s_xh, t + 1)
                dve.tensor_tensor(xl[:, q, :], bank[4 + q][:, 0:TS], xh[:, q, :], ALU.subtract).then_inc(s_xlo, 1)

            def cut_h(t, q, fresh=False):
                if not fresh:
                    dve.wait_ge(s_y, t - 1)
                for half in range(2):
                    hb = slice(half * HB // 2, (half + 1) * HB // 2)
                    dve.wait_ge(s_relu, t * HB + (half + 1) * HB // 2)
                    dve.tensor_copy(hh[:, q, hb, :], relu[:, q, hb, :]).then_inc(s_hs, 1)
                    dve.wait_ge(s_hs, t * 4 + half * 2 + 1)
                    dve.tensor_tensor(hl[:, q, hb, :], relu[:, q, hb, :], hh[:, q, hb, :], ALU.subtract
                                      ).then_inc(s_hs, 1)

            cut_x(0, 0)
            cut_x(1, 1)
            for t in range(2):
                cut_h(t, t, fresh=True)
                cut_x(t + 2, t)
            with dve.Fori(1, NT // 2) as g:
                for u in range(2):
                    cut_h(g * 2 + u, u)
                    cut_x(g * 2 + u + 2, u)

            for g in range(NK):
                xb = xres[:, g * CK:(g + 1) * CK, :]
                dve.wait_ge(s_yl[g % 2], (g // 2 + 1) * 32)
                link(dve.tensor_tensor(xb, xb, yin[:, g % 2, 0, :, :], ALU.add))
                dve.tensor_tensor(xb, xb, yin[:, g % 2, 1, :, :], ALU.add).then_inc(s_sum, 1)

        @block.scalar
        def _(act):
            act.wait_ge(s_w, 64)
            for g in range(NK):
                act.wait_ge(s_proj, g + 1)
                if g >= 2:
                    act.wait_ge(s_gp, g - 1)
                act.activation(h2t[:, g % 2, :], bank[6 + g % 2][:, :], ACT.Tanh, bias=bp_sb[:, 0:1]).then_inc(s_h2, 1)

            def tanh_blocks(pb, first=False):
                for m in range(2 * NK):
                    n = pb * 2 * NK + m
                    b = m % NBUF
                    act.wait_ge(s_sq, n + 1)
                    if not (first and m < NBUF):
                        act.wait_ge(s_pe, n - NBUF + 1)
                        act.wait_ge(s_ind, n - NBUF + 1)
                    act.activation(tbuf[:, b, :, :], abuf[:, b, :, :], ACT.Tanh).then_inc(s_t, 1)
                    if m % NK == 1 and not (first and m == 1):
                        feat_out(pb * 2 + m // NK - 1, (m // NK - 1) % 2)

            def feat_out(ib, parity):
                act.wait_ge(s_pe, (ib + 1) * NK)
                act.activation(feat_t[:, bass.ds(ib * IW, IW)], ps_feat[parity][:, :], ACT.Relu,
                               bias=bg_sb[:, 0:1]).then_inc(s_ev, 1)

            act.wait_ge(s_gp, NK)
            tanh_blocks(0, first=True)
            with act.Fori(1, NB // 2) as pb:
                tanh_blocks(pb)
            feat_out(NB - 1, 1)

            act.wait_ge(s_nr, 1)
            rounds = act.value_load(nrounds[0:1, 0:1], min_val=1, max_val=N // R)
            with act.Fori(0, rounds) as r:
                act.wait_ge(s_rsq, r + 1)
                act.activation(rowval[:, :], rowval[:, :], ACT.Tanh).then_inc(s_val, 1)
                act.wait_ge(s_fmm, r + 1)
                act.activation(fixed[:, :], ps_fix, ACT.Relu, bias=bg_sb[:, 0:1]).then_inc(s_fix, 1)

            def copy_norm(b):
                q = b % 2
                act.wait_ge(s_r2, b + 1)
                if b:
                    act.wait_ge(s_r3, b)
                act.activation(xnt, ps_xn[:, :], ACT.Copy).then_inc(s_xt, 1)
                if b >= 2:
                    act.wait_ge(s_scat[q], b // 2 * Q * 16)
                act.activation(aug[:, q, 1, :, 0:D], aug[:, q, 0, :, 0:D], ACT.Copy).then_inc(s_ax, 1)

            def exp_diff(b):
                act.wait_ge(s_df, b + 1)
                act.activation(ex[:, :], ex[:, :], ACT.Exp).then_inc(s_ex, 1)

            act.wait_ge(s_split, 2)
            for b in range(NB):
                copy_norm(b)
                if b:
                    exp_diff(b - 1)
            exp_diff(NB - 1)

            def upper_x(t, q, fresh=False):
                act.wait_ge(s_xp, t + 1)
                if not fresh:
                    act.wait_ge(s_h, (t - 1) * HB)
                act.activation(xh[:, q, :], bank[4 + q][:, 0:TS], ACT.Copy).then_inc(s_xh, 1)

            def relu_h(t, q, fresh=False):
                if not fresh:
                    act.wait_ge(s_hs, (t - 1) * 4)
                    act.sem_inc(s_spare, 1)
                e = act.value_load(tile_ei[0:1, bass.ds(t, 1)], min_val=0, max_val=E - 1)
                for hb in range(HB):
                    if hb % 2 == 0:
                        act.wait_ge(s_h, t * HB + hb + 2)
                    act.activation(relu[:, q, hb, :], bank[2 * q + hb // 2][:, hb % 2 * TS:(hb % 2 + 1) * TS],
                                   ACT.Relu, bias=b1_sb[:, bass.ds(e * HB + hb, 1)], scale=1.0 / WS
                                   ).then_inc(s_relu, 1)

            def y_out(t, u, q):
                act.wait_ge(s_y, t + 1)
                for s in range(2):
                    last = act.activation(ysb[:, u, s, :], bank[6 + q][:, s * D:(s + 1) * D], ACT.Copy,
                                          scale=xld[:, u, s, D + 1:D + 2])
                last.then_inc(s_yo, 1)

            act.wait_ge(s_tab, 1)
            upper_x(0, 0, fresh=True)
            upper_x(1, 1, fresh=True)

            def ffn_tiles(g, first):
                for u in range(NX):
                    t = g * NX + u
                    relu_h(t, u % 2, fresh=first and u < 2)
                    upper_x(t + 2, u % 2)
                    if u:
                        y_out(t - 1, u - 1, (u - 1) % 2)
                y_out(g * NX + NX - 1, NX - 1, (NX - 1) % 2)

            ffn_tiles(0, True)
            with act.Fori(1, NT // NX) as g:
                ffn_tiles(g, False)

            for g in range(NK):
                act.wait_ge(s_sum, g + 1)
                act.dma_start(out[g * IW:(g + 1) * IW, :].rearrange("(c p) d -> p c d", p=P),
                              xres[:, g * CK:(g + 1) * CK, :]).then_inc(s_out, 16)

        @block.tensor
        def _(pe):
            def transposes(src, dst, done):
                for cc in range(CK):
                    last = pe.transpose(dst[:, cc * P:(cc + 1) * P], src(cc), ident[:, :])
                last.then_inc(done, 1)

            pe.wait_ge(s_ident, 1)
            pe.wait_ge(s_w, 64)

            def project(g):
                pe.wait_ge(s_trc, g + 1)
                if g >= 2:
                    pe.wait_ge(s_h2, g - 1)
                pe.matmul(bank[6 + g % 2][:, :], wp_sb[:, :], xnorm_t[:, g * IW:(g + 1) * IW],
                          start=True, stop=True).then_inc(s_proj, 1)

            def make_g(g):
                pe.wait_ge(s_h2, g + 1)
                if g >= 2:
                    pe.wait_ge(s_g, g - 1)
                for cc in range(CK):
                    last = pe.matmul(ps_feat[g % 2][:, cc * P:(cc + 1) * P], h2t[:, g % 2, cc * P:(cc + 1) * P],
                                     wg_sb[:, :], start=True, stop=True)
                last.then_inc(s_gp, 1)

            for g in range(NK):
                pe.wait_ge(s_xn1, g + 1)
                if g >= 2:
                    pe.wait_ge(s_trc, g - 1)
                transposes(lambda cc: xnorm[:, g * CK + cc, :], [ps_x2, ps_xn][g % 2], s_tr)
                project(g)
                if g:
                    make_g(g - 1)
            make_g(NK - 1)
            pe.wait_ge(s_g, NK)
            pe.wait_ge(s_const, 1)

            def gnn_blocks(pb, first=False):
                for m in range(2 * NK):
                    n = pb * 2 * NK + m
                    b, half, k = m % NBUF, m // NK, m % NK
                    if k == 0 and not first:
                        pe.wait_ge(s_ev, pb * 2 + half - 1)
                        pe.wait_ge(s_cnt, pb * 2 + half - 1)
                    pe.wait_ge(s_t, n + 1)
                    for cc in range(CK):
                        c = k * CK + cc
                        pe.matmul(ps_feat[half][:, :], g_sb[:, c, :], tbuf[:, b, cc, :],
                                  start=(c == 0), stop=(c == C - 1))
                    pe.wait_ge(s_ind, n + 1)
                    for cc in range(CK):
                        c = k * CK + cc
                        for s in range(SUB):
                            last = pe.matmul(ps_cnt[half][:, s:s + 1], ind[:, b, cc, s * P:(s + 1) * P],
                                             ones_bf[:, 0:1], start=(c == 0 and s == 0), stop=(c == C - 1),
                                             skip_group_check=True)
                    last.then_inc(s_pe, 1)

            gnn_blocks(0, first=True)
            with pe.Fori(1, NB // 2) as pb:
                gnn_blocks(pb)

            pe.wait_ge(s_nr, 1)
            rounds = pe.value_load(nrounds[0:1, 0:1], min_val=1, max_val=N // R)
            TOTS = STEPS + 1
            with pe.Fori(0, rounds) as r:
                for b in range(STEPS):
                    pe.wait_ge(s_part, r * TOTS + b + 1)
                    pe.matmul(ps_ncand, same_row[:, :], ncand[:, :], start=True, stop=True).then_inc(s_tot, 1)
                pe.wait_ge(s_part, (r + 1) * TOTS)
                pe.matmul(ps_tie[:, 0:1], same_row[:, :], pair[:, 0:1], start=True, stop=True)
                pe.matmul(ps_tie[:, 1:2], before_row[:, :], pair[:, 1:2], start=True, stop=True
                          ).then_inc(s_tot, 1)
                pe.wait_ge(s_keep, r + 1)
                pe.transpose(ps_rowt, rowgt[:, :], ident[:, :]).then_inc(s_rt, 1)
                pe.wait_ge(s_rtc, r + 1)
                for c in range(C):
                    last = pe.matmul(ps_fix, g_sb[:, c, :], row_t[:, c::SEG], start=(c == 0), stop=(c == C - 1))
                last.then_inc(s_fmm, 1)

            def features_back(b):
                pe.wait_ge(s_ev, b + 1)
                if b:
                    pe.wait_ge(s_x2, b)
                transposes(lambda cc: feat_t[:, (b * SUB + cc) * P:(b * SUB + cc + 1) * P], ps_x2, s_r1)

            def normal_transpose(b):
                pe.wait_ge(s_xn, b + 1)
                if b:
                    pe.wait_ge(s_xt, b)
                transposes(lambda cc: aug[:, b % 2, 0, cc, 0:D], ps_xn, s_r2)

            def gate(b):
                pe.wait_ge(s_xt, b + 1)
                if b:
                    pe.wait_ge(s_gc, b)
                for cc in range(SUB):
                    dst = ps_gate[:, cc * E:(cc + 1) * E]
                    pe.matmul(dst, xnt[:, cc * P:(cc + 1) * P], gate_w[:, :], start=True, stop=False)
                    last = pe.matmul(dst, ones_f[0:1, :], gate_b[0:1, :], start=False, stop=True)
                last.then_inc(s_r3, 1)

            def places(b):
                pe.wait_ge(s_oh, b + 1)
                if b:
                    pe.wait_ge(s_sl, b)
                pe.matmul(ps_place, before[:, :], oh[:, :, :], start=True, stop=False, skip_group_check=True)
                for j in range(Q - 1):
                    n = Q - 1 - j
                    pe.matmul(ps_place[:, j + 1:, :], ones_bf[:, :],
                              oh[:, j:j + 1, :].to_broadcast([P, n, E]), start=False, stop=(j == Q - 2),
                              skip_group_check=True)
                for j in range(Q):
                    last = pe.matmul(ps_total, ones_bf[:, :], oh[:, j, :], start=(j == 0), stop=(j == Q - 1))
                last.then_inc(s_r4, 1)

            pe.wait_ge(s_ev, NB)
            pe.wait_ge(s_fixed, 1)
            pe.wait_ge(s_small, 80)
            for b in range(NB):
                features_back(b)
                normal_transpose(b)
                gate(b)
                if b:
                    places(b - 1)
            places(NB - 1)

            pe.wait_ge(s_split, 2)
            pe.wait_ge(s_tab, 1)

            def turn_x(t, u, fresh=False, round_=0):
                pe.wait_ge(s_xl[u], round_ * 16 + 16)
                if not fresh:
                    pe.wait_ge(s_xlo, t - 1)
                for s in range(2):
                    last = pe.transpose(bank[4 + u % 2][:, s * P:(s + 1) * P], xld[:, u, s, 0:D], ident[:, :])
                last.then_inc(s_xp, 1)

            def layer1(t, q, fresh=False):
                e = pe.value_load(tile_ei[0:1, bass.ds(t, 1)], min_val=0, max_val=E - 1)
                pe.wait_ge(s_xlo, t + 1)
                for hb in range(HB):
                    if not fresh and hb % 2 == 0:
                        pe.wait_ge(s_relu, (t - 2) * HB + hb + 2)
                    dst = bank[2 * q + hb // 2][:, hb % 2 * TS:(hb % 2 + 1) * TS]
                    hi = w1h[:, bass.ds(e, 1), hb * P:(hb + 1) * P].rearrange("p o h -> p (o h)")
                    lo = w1l[:, bass.ds(e, 1), hb * P:(hb + 1) * P].rearrange("p o h -> p (o h)")
                    pe.matmul(dst, hi, xh[:, q, :], start=True, stop=False)
                    pe.matmul(dst, hi, xl[:, q, :], start=False, stop=False)
                    pe.matmul(dst, lo, xh[:, q, :], start=False, stop=True).then_inc(s_h, 1)

            def layer2(t, q, fresh=False):
                e = pe.value_load(tile_ei[0:1, bass.ds(t, 1)], min_val=0, max_val=E - 1)
                if not fresh:
                    pe.wait_ge(s_yo, t - 1)
                for hb in range(HB):
                    if hb % 2 == 0:
                        pe.wait_ge(s_hs, t * 4 + hb + 2)
                    hi = w2h[:, bass.ds(e, 1), hb, :].rearrange("p o d -> p (o d)")
                    lo = w2l[:, bass.ds(e, 1), hb, :].rearrange("p o d -> p (o d)")
                    for s in range(2):
                        dst = bank[6 + q][:, s * D:(s + 1) * D]
                        hs, ls = hh[:, q, hb, s * P:(s + 1) * P], hl[:, q, hb, s * P:(s + 1) * P]
                        pe.matmul(dst, hs, hi, start=(hb == 0 and s == 0), stop=False, skip_group_check=True)
                        pe.matmul(dst, hs, lo, start=False, stop=False, skip_group_check=True)
                        pe.matmul(dst, ls, hi, start=False, stop=False, skip_group_check=True)
                for s in range(2):
                    last = pe.matmul(bank[6 + q][:, s * D:(s + 1) * D], ones_h[:, :],
                                     b2_hl[:, bass.ds(e, 1), :].rearrange("p o d -> p (o d)"),
                                     start=False, stop=True, skip_group_check=True)
                last.then_inc(s_y, 1)

            turn_x(0, 0, fresh=True)
            turn_x(1, 1, fresh=True)
            layer1(0, 0, fresh=True)

            def ffn_tiles(g, first):
                for u in range(NX):
                    t = g * NX + u
                    layer1(t + 1, (u + 1) % 2, fresh=first and u < 1)
                    turn_x(t + 2, (u + 2) % NX, round_=g + (u + 2) // NX)
                    layer2(t, u % 2, fresh=first and u < 2)

            ffn_tiles(0, True)
            with pe.Fori(1, NT // NX) as g:
                ffn_tiles(g, False)


def kernel(**inputs):
    import concourse.bacc as bacc
    from concourse.bass_utils import run_bass_kernel_spmd

    a = {k: np.asarray(v) for k, v in inputs.items()}
    adj = a["adj"]
    N = adj.shape[0]
    C = N // P
    w1, w2, b1 = a["L0_ffn_W1"], a["L0_ffn_W2"], a["L0_ffn_b1"]
    E, H, D = w1.shape
    laid = {
        "x": a["x"],
        "adj_tiles": adj.reshape(N // IW, IW, C // CK, CK, P).transpose(0, 2, 4, 3, 1),
        "adj_rows": adj,
        "w_proj": a["L0_gnn_W_proj"], "b_proj": a["L0_gnn_b_proj"],
        "w_gcn": a["L0_gnn_W_gcn"], "b_gcn": a["L0_gnn_b_gcn"],
        "w_gate": a["L0_ffn_Wg"].T, "b_gate": a["L0_ffn_bg"],
        "w1": w1.transpose(2, 0, 1),
        "b1": b1.reshape(E * (H // P), P).T,
        "w2": w2.reshape(E, D, H // P, P).transpose(3, 0, 2, 1),
        "b2": a["L0_ffn_b2"],
    }
    nc = bacc.Bacc("TRN2", target_bir_lowering=False, num_devices=1)
    arrays, args = {}, []
    for name, v in laid.items():
        v = np.ascontiguousarray(v)
        arrays["in_" + name] = v
        args.append(nc.dram_tensor("in_" + name, v.shape, mybir.dt.from_np(v.dtype), kind="ExternalInput").ap())
    res = nc.dram_tensor("out_0", a["x"].shape, mybir.dt.float32, kind="ExternalOutput").ap()
    gnn_moe_layer(nc, *args, res)
    r = run_bass_kernel_spmd(nc, [arrays], core_ids=[0])
    return r.results[0]["out_0"]
```

```python
import numpy as np
import concourse.bass as bass
from concourse import mybir
from contextlib import ExitStack

P = 128
IW = 512
CK = 4
WS = 128.0
ROW = 130
TS = 256


def gnn_moe_layer(nc, x, adj_tiles, adj_rows, w_proj, b_proj, w_gcn, b_gcn,
                  w_gate, b_gate, w1, b1, w2, b2, out):
    fp32, bf16, fp16, i32 = mybir.dt.float32, mybir.dt.bfloat16, mybir.dt.float16, mybir.dt.int32
    ALU, ACT, AX = mybir.AluOpType, mybir.ActivationFunctionType, mybir.AxisListType

    N, D = x.shape
    C = N // P
    TOPK = 350
    EPS = 1e-5
    E, H = b2.shape[0], w1.shape[2]
    HB = H // P
    NB = N // IW
    NK = C // CK
    NBUF = 4
    R = 4
    SEG = P // R
    STEPS = 15
    SUB = IW // P
    PIECES = [(0, C // 2), (C // 2, C)]
    Q = 2 * SUB
    RS = N + TS
    NT = 2 * N // TS + E
    NX = 8
    AHEAD = 2
    NCH = NB * NK
    ORDER = list(range(1, NB // 2 + 1)) + [0] + list(range(NB // 2 + 1, NB))
    START = [19, 27, 35, 43, 49, 55, 60, 67]
    AT_ADD, AT_NORM, AT_TURN, AT_COPY, AT_GATE = 2, 4, 4, 6, 6
    AT_CHOOSE, AT_SECOND, AT_EXP, AT_PLACE, AT_PROB, AT_ASSIGN = 8, 9, 9, 9, 11, 11
    OUT = 3
    FIX = NK + OUT + 1
    STEP0 = FIX + 7
    TIE = STEP0 + STEPS
    END = START[-1] + 14
    NOWHERE = 1 << 20

    xs = nc.dram_tensor("routed_rows", (E * RS + TS, ROW), fp32).ap()
    ys = nc.dram_tensor("expert_rows", (2 * N, D), fp32).ap()

    ctx = ExitStack()
    with ctx:
        ctx.enter_context(nc.allow_low_precision(reason="counts of at most 128 are exact"))

        def sb(name, shape, dt=fp32):
            return ctx.enter_context(nc.sbuf_tensor(name, shape, dt))

        def sem(name):
            return ctx.enter_context(nc.semaphore(name))

        xres = sb("xres", [P, C, D])
        g_sb = sb("g_sb", [P, C, D])
        feat_t = sb("feat_t", [P, N])
        w1h, w1l = sb("w1h", [P, E, H], fp16), sb("w1l", [P, E, H], fp16)
        w2h, w2l = sb("w2h", [P, E, HB, D], fp16), sb("w2l", [P, E, HB, D], fp16)
        wstage = sb("wstage", [P, E * H // 2])
        abuf = sb("abuf", [P, NBUF, CK, IW])
        tbuf = sb("tbuf", [P, NBUF, CK, IW])
        ind = sb("ind", [P, NBUF, CK, IW], bf16)
        aug = sb("aug", [P, 2, 2, SUB, ROW])
        xnt = sb("xnt", [P, IW])

        t_flat = tbuf[:, :, :, :].rearrange("p a b c -> p (a b c)")
        HC = C // 2
        xnorm = [w.bitcast(fp32).rearrange("p (c d) -> p c d", d=D)
                 for w in (w2h[:, :, :, :].rearrange("p e b d -> p (e b d)"),
                           w2l[:, :, :, :].rearrange("p e b d -> p (e b d)"))]
        xnorm_t = feat_t
        h2t = aug[:, :, :, :, :].rearrange("p a b c d -> p (a b c d)")[:, 0:2 * IW].rearrange("p (a i) -> p a i", a=2)
        a_flat = abuf[:, :, :, :].rearrange("p a b c -> p (a b c)")
        xld = a_flat[:, 0:NX * 2 * ROW].rearrange("p (n s w) -> p n s w", n=NX, s=2)
        ysb = a_flat[:, 2560:2560 + NX * TS].rearrange("p (n s d) -> p n s d", n=NX, s=2)
        relu = t_flat[:, 0:2 * HB * TS].rearrange("p (q h s) -> p q h s", q=2, h=HB)
        yin = t_flat.rearrange("p (g k c d) -> p g k c d", g=NK, k=2, d=D)
        t_half = t_flat[:, 2 * HB * TS:].bitcast(fp16)
        hh = t_half[:, 0:2 * HB * TS].rearrange("p (q h s) -> p q h s", q=2, h=HB)
        hl = t_half[:, 2 * HB * TS:4 * HB * TS].rearrange("p (q h s) -> p q h s", q=2, h=HB)
        xh = t_half[:, 4 * HB * TS:4 * HB * TS + 2 * TS].rearrange("p (q s) -> p q s", q=2)
        xl = t_half[:, 4 * HB * TS + 2 * TS:4 * HB * TS + 4 * TS].rearrange("p (q s) -> p q s", q=2)

        ident = sb("ident", [P, P])
        ones_f = sb("ones_f", [P, P])
        ones_bf = sb("ones_bf", [P, P], bf16)
        before = sb("before", [P, P], bf16)
        same_row = sb("same_row", [P, P], bf16)
        before_row = sb("before_row", [P, P], bf16)
        ones_h = sb("ones_h", [2, P], fp16)
        wp_sb = sb("wp_sb", [P, D])
        wg_sb = sb("wg_sb", [P, D])
        bp_sb = sb("bp_sb", [P, 1])
        bg_sb = sb("bg_sb", [P, 1])
        gate_w = sb("gate_w", [P, E])
        gate_b = sb("gate_b", [P, E])
        b1_sb = sb("b1_sb", [P, E * HB])
        b2_f = sb("b2_f", [2, E, D])
        b2_h = sb("b2_h", [2, E, D], fp16)
        b2_hl = sb("b2_hl", [2, E, D], fp16)
        pidx = sb("pidx", [P, 1], i32)
        is_p1 = sb("is_p1", [2, 1])
        is_p0 = sb("is_p0", [2, 1])
        stats = sb("stats", [P, C, 6])
        mean = sb("mean", [P, C])
        var = sb("var", [P, C])
        rstd = sb("rstd", [P, C])
        tmp = sb("tmp", [P, C])
        rowid = sb("rowid", [P, C], i32)
        rowidf = sb("rowidf", [P, C])
        count = sb("count", [P, C])
        key = sb("key", [P, C])
        keyrow = t_flat[0:1, 0:N]
        keyflag = t_flat[0:1, N:2 * N]
        key0 = sb("key0", [P, SUB])
        keyrow0 = sb("keyrow0", [1, IW])
        flags = sb("flags", [P, C])
        flagged = sb("flagged", [P, 2], bf16)
        nflags = sb("nflags", [1, 2])
        redo_i = sb("redo_i", [1, 1], i32)
        nflag = sb("nflag", [1, 1])
        nrounds = sb("nrounds", [1, 1], i32)
        top = sb("top", [1, 8])
        ids = sb("ids", [1, 8], i32)
        rowval = sb("rowval", [P, P])
        rowsc = sb("rowsc", [P, P])
        rowbf = sb("rowbf", [P, 4, P], bf16)
        rowgt = sb("rowgt", [P, P])
        roweq = sb("roweq", [P, P])
        row_t = sb("row_t", [P, P])
        bits = sb("bits", [P, STEPS, 4], i32)
        thr = sb("thr", [P, 1])
        cand = sb("cand", [P, 4], i32)
        ncand = sb("ncand", [P, 4], bf16)
        okc = sb("okc", [P, 4])
        pair = sb("pair", [P, 2], bf16)
        need = sb("need", [P, 1])
        fixrow = sb("fixrow", [P, D])
        fixed = sb("fixed", [P, R])
        scores = sb("scores", [P, SUB, E])
        masked = sb("masked", [P, SUB, E])
        hit = sb("hit", [P, SUB, E])
        oh = sb("oh", [P, Q, E], bf16)
        eidx = sb("eidx", [P, SUB, E])
        eidx_i = sb("eidx_i", [P, SUB, E], i32)
        m1 = sb("m1", [P, SUB])
        m2 = sb("m2", [P, SUB])
        pick = sb("pick", [P, SUB])
        ex = sb("ex", [P, SUB])
        p1 = sb("p1", [P, SUB])
        dest = sb("dest", [P, 2, C], i32)
        place = sb("place", [P, Q, E])
        slots = sb("slots", [P, 2, Q], i32)
        base = sb("base", [P, E])
        base_i = sb("base_i", [P, E], i32)
        pad = sb("pad", [P, 2, ROW])
        tnum_i = sb("tnum_i", [1, NT + AHEAD, E], i32)
        tnum = sb("tnum", [1, NT + AHEAD, E])
        table = wstage[0:1, :].rearrange("o (k t e) -> o k t e", e=E, k=2)
        past = table[:, 0, 0:NT + AHEAD, :]
        jump = table[:, 1, 0:NT + AHEAD, :]
        tiles = sb("tiles", [1, E])
        tiles_i = sb("tiles_i", [1, E], i32)
        ends = sb("ends", [1, E])
        skip = sb("skip", [1, E])
        tile_e = sb("tile_e", [1, NT + AHEAD])
        tile_ei = sb("tile_ei", [1, NT + AHEAD], i32)
        tile_r = sb("tile_r", [1, NT + AHEAD])
        tile_ri = sb("tile_ri", [1, NT + AHEAD], i32)
        pad_i = sb("pad_i", [1, E], i32)

        bank = [ctx.enter_context(nc.psum_tensor(f"bank{i}", [P, 512], fp32)) for i in range(8)]
        ps_feat, ps_cnt = bank[0:2], bank[2:4]
        ps_x2, ps_xn = bank[4], bank[5]
        ps_gate = bank[6][:, 0:SUB * E]
        ps_place = bank[6][:, 64:64 + Q * E].rearrange("p (q e) -> p q e", e=E)
        ps_total = bank[6][:, 64 + Q * E:64 + Q * E + E]
        ps_ncand = bank[7][:, 0:4]
        ps_tie = bank[7][:, 8:10]
        ps_flag = bank[7][:, 16:18]
        ps_rowt = bank[7][:, 128:256]
        ps_fixrow = bank[7][0:R, 256:256 + D]
        ps_fixt = bank[7][:, 384:384 + P]

        s_x = [sem(f"s_xpiece{i}") for i in range(len(PIECES))]
        s_w = sem("s_w")
        s_small = sem("s_small")
        s_wst = sem("s_wst")
        s_split = sem("s_split")
        s_const = sem("s_const")
        s_ident = sem("s_ident")
        s_pool = sem("s_pool")
        s_dve = sem("s_dve")
        s_xn1 = sem("s_xn1")
        s_tr = sem("s_tr")
        s_trc = sem("s_trc")
        s_proj = sem("s_proj")
        s_h2 = sem("s_h2")
        s_gp = sem("s_gp")
        s_g = sem("s_g")
        s_a = [sem(f"s_a{i}") for i in range(NBUF)]
        s_sq = sem("s_sq")
        s_t = sem("s_t")
        s_ind = sem("s_ind")
        s_pe = sem("s_pe")
        s_ev = sem("s_ev")
        s_cnt = sem("s_cnt")
        s_redo = sem("s_redo")
        s_flagged = sem("s_flagged")
        s_nflags = sem("s_nflags")
        s_key = sem("s_key")
        s_keyrow = sem("s_keyrow")
        s_nr = sem("s_nr")
        s_fixed = sem("s_fixed")
        s_xre = sem("s_xre")
        s_dve2 = sem("s_dve2")
        s_key0 = sem("s_key0")
        s_keyrow0 = sem("s_keyrow0")
        s_spare = sem("s_spare")

        class RoundSems:
            def __init__(self, v):
                self.ids = sem("s_ids" + v)
                self.rows = sem("s_rows" + v)
                self.chain = sem("s_fdve" + v)
                self.rsq = sem("s_rsq" + v)
                self.val = sem("s_val" + v)
                self.part = sem("s_part" + v)
                self.tot = sem("s_tot" + v)
                self.keep = sem("s_keep" + v)
                self.rt = sem("s_rt" + v)
                self.rtc = sem("s_rtc" + v)
                self.fmm = sem("s_fmm" + v)
                self.frow = sem("s_frow" + v)
                self.ft = sem("s_ft" + v)
                self.fix = sem("s_fix" + v)

        class RouteSems:
            def __init__(self, v):
                self.r1 = sem("s_r1" + v)
                self.x2 = sem("s_x2" + v)
                self.st = sem("s_st" + v)
                self.ns = sem("s_ns" + v)
                self.xn = sem("s_xn" + v)
                self.r2 = sem("s_r2" + v)
                self.xt = sem("s_xt" + v)
                self.ax = sem("s_ax" + v)
                self.r3 = sem("s_r3" + v)
                self.score = sem("s_score" + v)
                self.df = sem("s_df" + v)
                self.ex = sem("s_ex" + v)
                self.oh = sem("s_oh" + v)
                self.meta = sem("s_meta" + v)
                self.r4 = sem("s_r4" + v)
                self.sl = sem("s_sl" + v)
                self.scat = [sem(f"s_scat{i}" + v) for i in range(2)]

        early, general = RoundSems("_early"), RoundSems("_general")
        routed, rerouted = RouteSems(""), RouteSems("_again")
        fixed_early = sem("s_fixed_early")
        s_padb = sem("s_padb")
        s_padd = sem("s_padd")
        s_padr = sem("s_padr")
        s_tab = sem("s_tab")
        s_pads = sem("s_pads")
        s_xl = [sem(f"s_xl{i}") for i in range(NX)]
        s_xp = sem("s_xp")
        s_xh = sem("s_xh")
        s_xlo = sem("s_xlo")
        s_h = sem("s_h")
        s_relu = sem("s_relu")
        s_hs = sem("s_hs")
        s_y = sem("s_y")
        s_yo = sem("s_yo")
        s_sc = [sem(f"s_sc{i}") for i in range(NX)]
        s_yl = [sem(f"s_yl{i}") for i in range(NK)]
        s_sum = sem("s_sum")
        s_out = sem("s_out")

        def fetch_rows(eng, f, r):
            eng.wait_ge(f.ids, r + 1)
            eng.sem_inc(s_spare, 1)
            for q in range(R):
                row = eng.value_load(ids[0:1, q:q + 1], min_val=0, max_val=N - 1)
                eng.dma_start(rowval[q * SEG:(q + 1) * SEG, :], adj_rows[bass.ds(row, 1), :]
                              .rearrange("o (s f) -> s (o f)", s=SEG)).then_inc(f.rows, 16)

        def load_experts(nc, eng, g, n):
            return nc.values_load_multi_w_load_instructions(
                tile_ei[0:1, bass.ds(g * NX, n)], engines=[eng.engine], min_val=0, max_val=E - 1,
                skip_runtime_bounds_check_because="tile_ei is min(count, E - 1) of nonnegative counts")[1]

        def read_redo(eng):
            eng.wait_ge(s_redo, 1)
            eng.sem_inc(s_spare, 1)
            return eng.value_load(redo_i[0:1, 0:1], min_val=0, max_val=N)

        def read_rounds(eng):
            eng.wait_ge(s_nr, 1)
            eng.sem_inc(s_spare, 1)
            return eng.value_load(nrounds[0:1, 0:1], min_val=1, max_val=N // R)

        def norm_scale(eng, link, c0, n):
            st, mn, vr, rs, tp = (a[:, c0:c0 + n] for a in (stats, mean, var, rstd, tmp))
            eng.tensor_tensor(mn, st[:, :, 1], st[:, :, 4], ALU.add)
            eng.tensor_tensor(vr, st[:, :, 2], st[:, :, 5], ALU.add)
            link(eng.tensor_tensor(tp, st[:, :, 1], st[:, :, 4], ALU.subtract))
            eng.tensor_scalar(mn, mn, 0.5, None, ALU.mult)
            eng.tensor_scalar(vr, vr, 1.0 / D, EPS, ALU.mult, ALU.add)
            link(eng.tensor_tensor(tp, tp, tp, ALU.mult))
            link(eng.tensor_scalar(tp, tp, 0.25, None, ALU.mult))
            link(eng.tensor_tensor(vr, vr, tp, ALU.add))
            link(eng.tensor_scalar(rs.bitcast(i32), vr.bitcast(i32), -0.5, float(0x5F3759DF), ALU.mult, ALU.add))
            link(eng.tensor_scalar(vr, vr, -0.5, None, ALU.mult))
            for step in range(3):
                link(eng.tensor_tensor(tp, rs, rs, ALU.mult))
                link(eng.tensor_tensor(tp, tp, vr, ALU.mult))
                link(eng.tensor_scalar(tp, tp, 1.5, None, ALU.add))
                last = eng.tensor_tensor(rs, rs, tp, ALU.mult)
                if step < 2:
                    link(last)
            return last

        block = ctx.enter_context(nc.Block())

        @block.sync
        def _(sp):
            for i, (c0, c1) in enumerate(PIECES):
                sp.dma_start(xres[:, c0:c1, :], x[c0 * P:c1 * P, :].rearrange("(c p) d -> p c d", p=P)
                             ).then_inc(s_x[i], 16)

            for n in range(NCH):
                if n >= NBUF:
                    sp.wait_ge(s_t, n - NBUF + 1)
                sp.dma_start(abuf[:, n % NBUF, :, :], adj_tiles[n // NK, n % NK, :, :, :]).then_inc(s_a[n % NBUF], 16)
            sp.wait_ge(s_padb, 1)
            sp.dma_start(xs[E * RS:E * RS + TS, :].rearrange("(s p) w -> p s w", p=P), pad[:, :, :]
                         ).then_inc(s_padd, 16)

            redo = read_redo(sp)
            with sp.If(redo > 0):
                sp.wait_ge(routed.xn, NB)
                sp.dma_start(xres[:, :, :], x.rearrange("(c p) d -> p c d", p=P)).then_inc(s_xre, 16)
                sp.wait_ge(s_key, 1)
                sp.dma_start(keyrow.rearrange("o (p t) -> o p t", p=P),
                             key[:, :].rearrange("p (o t) -> p o t", o=1)).then_inc(s_keyrow, 16)
                rounds = read_rounds(sp)
                with sp.Fori(0, rounds) as r:
                    fetch_rows(sp, general, r)
                for i in range(2):
                    sp.wait_ge(rerouted.scat[i], NB // 2 * Q * 16)

            sp.wait_ge(s_padr, 1)
            for e in range(E):
                row = sp.value_load(pad_i[0:1, e:e + 1], min_val=0, max_val=E * RS - TS)
                sp.dma_start(xs[bass.ds(row, TS), :].rearrange("(s p) w -> p s w", p=P), pad[:, :, :]
                             ).then_inc(s_pads, 16)
            sp.wait_ge(s_pads, 16 * E)
            sp.wait_ge(s_padd, 16)
            for i in range(2):
                sp.wait_ge(routed.scat[i], NB // 2 * Q * 16)
            sp.wait_ge(s_tab, 1)

            def load_tile(t, u, first=False):
                if not first:
                    sp.wait_ge(s_sc[u], (t - u) // NX * 32)
                    sp.sem_inc(s_spare, 1)
                row = sp.value_load(tile_ri[0:1, bass.ds(t, 1)], min_val=0, max_val=E * RS)
                sp.dma_start(xld[:, u, :, :], xs[bass.ds(row, TS), :].rearrange("(s p) w -> p s w", p=P)
                             ).then_inc(s_xl[u], 16)

            for u in range(NX):
                load_tile(u, u, first=True)
            with sp.Fori(1, NT // NX) as g:
                for u in range(NX):
                    sp.wait_ge(s_sc[u], g * 32)
                    sp.sem_inc(s_spare, 1)
                    row = sp.value_load(tile_ri[0:1, bass.ds(g * NX + u, 1)], min_val=0, max_val=E * RS)
                    sp.dma_start(xld[:, u, :, :], xs[bass.ds(row, TS), :].rearrange("(s p) w -> p s w", p=P)
                                 ).then_inc(s_xl[u], 16)
            for u in range(AHEAD):
                sp.wait_ge(s_sc[u], NT // NX * 32)
                row = sp.value_load(tile_ri[0:1, NT + u:NT + u + 1], min_val=0, max_val=E * RS)
                sp.dma_start(xld[:, u, :, :], xs[bass.ds(row, TS), :].rearrange("(s p) w -> p s w", p=P)
                             ).then_inc(s_xl[u], 16)

            for u in range(NX):
                sp.wait_ge(s_sc[u], NT // NX * 32)
            sp.wait_ge(s_h, (NT + 1) * HB)
            sp.wait_ge(s_xlo, NT + AHEAD)
            for g in range(NK):
                for k in range(2):
                    sp.dma_start(yin[:, g, k, :, :],
                                 ys[k * N + g * IW:k * N + (g + 1) * IW, :].rearrange("(c p) d -> p c d", p=P)
                                 ).then_inc(s_yl[g], 16)
            sp.wait_ge(s_out, NK * 16)

        @block.gpsimd
        def _(pool):
            links = [0]

            def link(ins):
                links[0] += 1
                ins.then_inc(s_pool, 1)
                pool.wait_ge(s_pool, links[0])

            link(pool.memset(ident[:, :], 0.0))
            pool.affine_select(out=ident[:, :], in_=ident[:, :], compare_op=ALU.not_equal, fill=1.0, base=0,
                               pattern=[[-1, P]], channel_multiplier=1).then_inc(s_ident, 1)
            pool.dma_start(b1_sb[:, :], b1).then_inc(s_small, 16)
            pool.dma_start(gate_w[:, :], w_gate).then_inc(s_small, 16)
            pool.dma_start(gate_b[:, :], b_gate.rearrange("(o e) -> o e", o=1).to_broadcast([P, E])).then_inc(s_small, 16)
            for i in range(2):
                pool.dma_start(b2_f[i:i + 1, :, :], b2.rearrange("(o e) d -> o e d", o=1)).then_inc(s_small, 16)
            pool.memset(ones_bf[:, :], 1.0)
            pool.memset(ones_f[:, :], 1.0)
            link(pool.memset(ones_h[:, :], 1.0))
            link(pool.affine_select(out=before[:, :], in_=ones_bf[:, :], compare_op=ALU.is_ge, fill=0.0, base=-1,
                                    pattern=[[1, P]], channel_multiplier=-1))
            grid = [[-SEG, R], [0, SEG]]
            link(pool.affine_select(out=same_row[:, :].rearrange("p (r s) -> p r s", r=R),
                                    in_=ones_bf[:, :].rearrange("p (r s) -> p r s", r=R),
                                    compare_op=ALU.is_ge, fill=0.0, base=0, pattern=grid, channel_multiplier=1))
            link(pool.affine_select(out=same_row[:, :].rearrange("p (r s) -> p r s", r=R),
                                    in_=same_row[:, :].rearrange("p (r s) -> p r s", r=R),
                                    compare_op=ALU.is_ge, fill=0.0, base=SEG - 1, pattern=[[SEG, R], [0, SEG]],
                                    channel_multiplier=-1))
            link(pool.tensor_tensor(before_row[:, :], before[:, :], same_row[:, :], ALU.mult))
            pool.iota(rowid[:, :], [[P, C]], base=1, channel_multiplier=1)
            pool.iota(dest[:, :, :], [[N, 2], [P, C]], base=0, channel_multiplier=1)
            pool.iota(eidx_i[:, :, :], [[0, SUB], [-1, E]], base=E, channel_multiplier=0)
            pool.iota(base_i[:, :], [[RS, E]], base=0, channel_multiplier=0)
            pool.iota(tnum_i[:, :, :], [[1, NT + AHEAD], [0, E]], base=0, channel_multiplier=0)
            link(pool.iota(pidx[:, :], [[0, 1]], base=0, channel_multiplier=1))
            for b in range(STEPS):
                for k in range(4):
                    pool.memset(bits[:, b, k:k + 1], k << (2 * (STEPS - 1 - b)))
            pool.memset(pad[:, :, :], 0.0)
            pool.memset(fixrow[:, :], 0.0)
            link(pool.memset(ncand[:, :], float(P)))
            pool.memset(pad[:, :, D:D + 1].bitcast(i32), NOWHERE).then_inc(s_padb, 1)
            pool.wait_ge(s_padb, 1)
            pool.tensor_copy(eidx[:, :, :], eidx_i[:, :, :])
            pool.tensor_copy(rowidf[:, :], rowid[:, :])
            pool.tensor_copy(base[:, :], base_i[:, :])
            pool.tensor_copy(tnum[:, :, :], tnum_i[:, :, :])
            link(pool.tensor_copy(is_p1[:, :], pidx[0:2, :]))
            link(pool.tensor_scalar(is_p0[:, :], is_p1[:, :], -1.0, 1.0, ALU.mult, ALU.add))
            pool.wait_ge(s_small, 80)
            link(pool.tensor_scalar(b2_f[:, :, :], b2_f[:, :, :], WS, 0.0, ALU.mult, ALU.add))
            link(pool.tensor_copy(b2_h[:, :, :], b2_f[:, :, :]))
            link(pool.tensor_tensor(b2_f[:, :, :], b2_f[:, :, :], b2_h[:, :, :], ALU.subtract))
            link(pool.tensor_scalar(b2_f[:, :, :], b2_f[:, :, :], is_p1[:, 0:1], 0.0, ALU.mult, ALU.add))
            link(pool.tensor_scalar(b2_hl[:, :, :], b2_h[:, :, :], is_p0[:, 0:1], 0.0, ALU.mult, ALU.add))
            pool.tensor_tensor(b2_hl[:, :, :], b2_hl[:, :, :], b2_f[:, :, :], ALU.add).then_inc(s_const, 1)

            def split_weights():
                halves = 0
                for src, hi, lo in ((w1.rearrange("p e h -> p (e h)"), w1h[:, :, :].rearrange("p e h -> p (e h)"),
                                     w1l[:, :, :].rearrange("p e h -> p (e h)")),
                                    (w2.rearrange("p e b d -> p (e b d)"),
                                     w2h[:, :, :, :].rearrange("p e b d -> p (e b d)"),
                                     w2l[:, :, :, :].rearrange("p e b d -> p (e b d)"))):
                    for half in range(2):
                        cols = slice(half * E * H // 2, (half + 1) * E * H // 2)
                        if halves:
                            pool.wait_ge(s_split, halves)
                        pool.dma_start(wstage[:, :], src[:, cols]).then_inc(s_wst, 16)
                        halves += 1
                        if halves == 3:
                            pool.wait_ge(s_tr, NK)
                        pool.wait_ge(s_wst, halves * 16)
                        link(pool.tensor_scalar(wstage[:, :], wstage[:, :], WS, 0.0, ALU.mult, ALU.add))
                        link(pool.tensor_copy(hi[:, cols], wstage[:, :]))
                        pool.tensor_tensor(lo[:, cols], wstage[:, :], hi[:, cols], ALU.subtract).then_inc(s_split, 1)

            def scatter(i, rs):
                pool.wait_ge(rs.sl, i + 1)
                pool.wait_ge(rs.meta, i + 1)
                pool.wait_ge(rs.ax, i + 1)
                for k in range(2):
                    for cc in range(SUB):
                        pool.indirect_dma_start(
                            xs, bass.IndirectOffsetOnAxis(ap=slots[:, i % 2, k * SUB + cc:k * SUB + cc + 1], axis=0),
                            aug[:, i % 2, k, cc, :], None).then_inc(rs.scat[i % 2], 16)

            def scale(i, b, rs):
                pool.wait_ge(rs.st, i + 1)
                norm_scale(pool, link, b * SUB, SUB).then_inc(rs.ns, 1)

            split_weights()
            for i, b in enumerate(ORDER):
                if i < NB - 1:
                    scale(i, b, routed)
                if i:
                    scatter(i - 1, routed)
            scatter(NB - 1, routed)
            redo = read_redo(pool)
            with pool.If(redo > 0):
                for b in range(NB):
                    scatter(b, rerouted)

            def store_tile(t, u, loop=True):
                pool.wait_ge(s_yo, t + 1)
                if loop:
                    pool.sem_inc(s_spare, 1)
                for s in range(2):
                    pool.indirect_dma_start(
                        ys, bass.IndirectOffsetOnAxis(ap=xld[:, u, s, D:D + 1].bitcast(i32), axis=0),
                        ysb[:, u, s, :], None, bounds_check=2 * N - 1, oob_is_err=False).then_inc(s_sc[u], 16)

            with pool.Fori(0, NT // NX) as g:
                for u in range(NX):
                    store_tile(g * NX + u, u)

        @block.vector
        def _(dve):
            chain = [s_dve, 0]

            def link(ins):
                chain[1] += 1
                ins.then_inc(chain[0], 1)
                dve.wait_ge(chain[0], chain[1])

            for i, (c0, c1) in enumerate(PIECES):
                dve.wait_ge(s_x[i], 16)
                for c in range(c0, c1):
                    last = dve.bn_stats(stats[:, c, :], xres[:, c, :])
                link(last)
                link(norm_scale(dve, link, c0, c1 - c0))
                for c in range(c0, c1):
                    ins = dve.tensor_scalar(xnorm[c // HC][:, c % HC, :], xres[:, c, :], mean[:, c:c + 1],
                                            rstd[:, c:c + 1], ALU.subtract, ALU.mult)
                    if c % CK == CK - 1:
                        ins.then_inc(s_xn1, 1)

            CHAIN = 2 + 3 * STEPS + 1 + 4 + R
            TOTS = STEPS + 1
            links = [0]

            def rlink(f, r, ins):
                links[0] += 1
                ins.then_inc(f.chain, 1)
                dve.wait_ge(f.chain, r * CHAIN + links[0])

            def pick_rows(f, r, row):
                links[0] = 0
                rlink(f, r, dve.max(top[:, :], row))
                dve.tensor_scalar(ids[:, :], top[:, :], -1.0, 0.0, ALU.add, ALU.max).then_inc(f.ids, 1)
                dve.scalar_tensor_tensor(row, row, top[:, R - 1:R], row, ALU.is_lt, ALU.mult)
                rlink(f, r, dve.memset(thr[:, :], 0.0))

            def square_rows(f, r):
                dve.wait_ge(f.rows, (r + 1) * 16 * R)
                dve.scalar_tensor_tensor(rowval[:, :], rowval[:, :], 0.0, rowval[:, :], ALU.max, ALU.mult
                                         ).then_inc(f.rsq, 1)

            def count_candidates(f, r, b):
                rlink(f, r, dve.tensor_tensor(cand[:, :], bits[:, b, :], thr[:, :].bitcast(i32).to_broadcast([P, 4]),
                                              ALU.bitwise_or))
                if b == 0:
                    dve.wait_ge(f.val, r + 1)
                for k in range(1, 4):
                    last = dve.tensor_scalar(rowbf[:, k, :], rowval[:, :], cand[:, k:k + 1].bitcast(fp32), None,
                                             ALU.is_ge, ALU.add, accum_out=ncand[:, k:k + 1])
                last.then_inc(f.part, 1)

            def raise_threshold(f, r, b):
                dve.wait_ge(f.tot, r * TOTS + b + 1)
                rlink(f, r, dve.scalar_tensor_tensor(okc[:, :], ps_ncand, float(TOPK), cand[:, :].bitcast(fp32),
                                                     ALU.is_ge, ALU.mult))
                rlink(f, r, dve.tensor_reduce(thr[:, :], okc[:, :], AX.X, ALU.max))

            def count_ties(f, r):
                dve.tensor_scalar(rowgt[:, :], rowval[:, :], thr[:, 0:1], None, ALU.is_gt, ALU.add,
                                  accum_out=pair[:, 0:1])
                dve.tensor_scalar(roweq[:, :], rowval[:, :], thr[:, 0:1], None, ALU.is_equal, ALU.add,
                                  accum_out=pair[:, 1:2]).then_inc(f.part, 1)
                dve.wait_ge(f.part, (r + 1) * TOTS)
                rlink(f, r, dve.tensor_tensor_scan(rowsc[:, :], ones_f[:, :], roweq[:, :], 0.0, ALU.mult, ALU.add))

            def mask_rows(f, r):
                dve.wait_ge(f.tot, (r + 1) * TOTS)
                rlink(f, r, dve.tensor_scalar(need[:, :], ps_tie[:, 0:1], -1.0, float(TOPK), ALU.mult, ALU.add))
                rlink(f, r, dve.tensor_tensor(need[:, :], need[:, :], ps_tie[:, 1:2], ALU.subtract))
                rlink(f, r, dve.scalar_tensor_tensor(roweq[:, :], rowsc[:, :], need[:, 0:1], roweq[:, :],
                                                     ALU.is_le, ALU.mult))
                rlink(f, r, dve.tensor_tensor(rowgt[:, :], rowgt[:, :], roweq[:, :], ALU.add))
                dve.tensor_tensor(rowgt[:, :], rowgt[:, :], rowval[:, :], ALU.mult).then_inc(f.keep, 1)

            def rows_turned(f, r):
                dve.wait_ge(f.rt, r + 1)
                dve.tensor_copy(row_t[:, :], ps_rowt).then_inc(f.rtc, 1)

            def write_features(f, r):
                dve.wait_ge(f.fix, r + 1)
                dve.sem_inc(s_spare, 1)
                rows = [dve.value_load(ids[0:1, q:q + 1], min_val=0, max_val=N - 1) for q in range(R)]
                for q in range(R):
                    rlink(f, r, dve.tensor_copy(feat_t[:, bass.ds(rows[q], 1)], fixed[:, q:q + 1]))
                assert links[0] == CHAIN, links

            def spread(v):
                return v[:, :].rearrange("p (c o) -> p c o", o=1).to_broadcast([P, SUB, E])

            def first_of_max(src, m, onehot):
                link(dve.tensor_reduce(m[:, :], src, AX.X, ALU.max))
                link(dve.tensor_tensor(hit[:, :, :], src, spread(m), ALU.is_equal))
                link(dve.tensor_tensor(hit[:, :, :], hit[:, :, :], eidx[:, :, :], ALU.mult))
                link(dve.tensor_reduce(pick[:, :], hit[:, :, :], AX.X, ALU.max))
                return dve.tensor_tensor(onehot, eidx[:, :, :], spread(pick), ALU.is_equal)

            def add_features(i, b, rs, scale=False):
                dve.wait_ge(rs.r1, i + 1)
                xb = xres[:, b * SUB:(b + 1) * SUB, :]
                dve.tensor_tensor(xb, xb, ps_x2[:, :].rearrange("p (c d) -> p c d", c=SUB), ALU.add
                                  ).then_inc(rs.x2, 1)
                dve.wait_ge(rs.x2, i + 1)
                for cc in range(SUB):
                    last = dve.bn_stats(stats[:, b * SUB + cc, :], xres[:, b * SUB + cc, :])
                if scale:
                    link(last)
                    last = norm_scale(dve, link, b * SUB, SUB)
                last.then_inc(rs.ns if scale else rs.st, 1)

            def normalise(i, b, rs):
                q = i % 2
                dve.wait_ge(rs.ns, i + 1)
                if i >= 2:
                    dve.wait_ge(rs.scat[q], i // 2 * Q * 16)
                for cc in range(SUB):
                    c = b * SUB + cc
                    last = dve.tensor_scalar(aug[:, q, 0, cc, 0:D], xres[:, c, :], mean[:, c:c + 1],
                                             rstd[:, c:c + 1], ALU.subtract, ALU.mult)
                last.then_inc(rs.xn, 1)

            def choose(i, b, rs):
                dve.wait_ge(rs.r3, i + 1)
                dve.tensor_tensor(scores[:, :, :], ps_gate.rearrange("p (c e) -> p c e", e=E),
                                  gate_b[:, :].rearrange("p (o e) -> p o e", o=1).to_broadcast([P, SUB, E]), ALU.add
                                  ).then_inc(rs.score, 1)
                dve.wait_ge(rs.score, i + 1)
                if i:
                    dve.wait_ge(rs.r4, i)
                link(first_of_max(scores[:, :, :], m1, oh[:, 0:SUB, :]))
                link(dve.scalar_tensor_tensor(masked[:, :, :], oh[:, 0:SUB, :], -3.0e38, scores[:, :, :],
                                              ALU.mult, ALU.add))

            def choose_second(i, b, rs):
                first_of_max(masked[:, :, :], m2, oh[:, SUB:Q, :]).then_inc(rs.oh, 1)
                dve.tensor_tensor(ex[:, :], m2[:, :], m1[:, :], ALU.subtract).then_inc(rs.df, 1)

            def probabilities(i, b, rs):
                q = i % 2
                for k in range(2):
                    dve.tensor_copy(aug[:, q, k, :, D].bitcast(i32), dest[:, k, b * SUB:(b + 1) * SUB])
                dve.wait_ge(rs.ex, i + 1)
                link(dve.tensor_scalar(p1[:, :], ex[:, :], 1.0, None, ALU.add))
                link(dve.reciprocal(p1[:, :], p1[:, :]))
                link(dve.tensor_scalar(p1[:, :], p1[:, :], 1.0 / WS, None, ALU.mult))
                dve.tensor_copy(aug[:, q, 0, :, D + 1], p1[:, :])
                dve.tensor_tensor(aug[:, q, 1, :, D + 1], ex[:, :], p1[:, :], ALU.mult).then_inc(rs.meta, 1)

            def assign(i, rs):
                q = i % 2
                dve.wait_ge(rs.r4, i + 1)
                link(dve.tensor_tensor(place[:, :, :], ps_place,
                                       base[:, :].rearrange("p (o e) -> p o e", o=1).to_broadcast([P, Q, E]), ALU.add))
                link(dve.tensor_tensor(place[:, :, :], place[:, :, :], oh[:, :, :], ALU.mult))
                if i >= 2:
                    dve.wait_ge(rs.scat[q], i // 2 * Q * 16)
                dve.tensor_reduce(slots[:, q, :], place[:, :, :], AX.X, ALU.add)
                dve.tensor_tensor(base[:, :], base[:, :], ps_total, ALU.add).then_inc(rs.sl, 1)
                dve.wait_ge(rs.sl, i + 1)

            def counts_out(ib):
                dve.wait_ge(s_pe, (ib + 1) * NK)
                dve.tensor_copy(count[:, ib * SUB:(ib + 1) * SUB], ps_cnt[ib % 2][:, 0:SUB]).then_inc(s_cnt, 1)

            for n in range(END):
                if n < NCH:
                    dve.wait_ge(s_a[n % NBUF], (n // NBUF + 1) * 16)
                    buf = abuf[:, n % NBUF, :, :]
                    dve.scalar_tensor_tensor(buf, buf, 0.0, buf, ALU.max, ALU.mult).then_inc(s_sq, 1)
                if n >= NK and n % NK == OUT:
                    if n // NK <= NB:
                        counts_out(n // NK - 1)
                if n == FIX:
                    dve.wait_ge(s_const, 1)
                    dve.wait_ge(s_cnt, 1)
                    link(dve.tensor_scalar(key0[:, :], count[:, 0:SUB], float(TOPK), None, ALU.is_gt))
                    dve.tensor_tensor(key0[:, :], key0[:, :], rowidf[:, 0:SUB], ALU.mult).then_inc(s_key0, 1)
                if n == FIX + 2:
                    dve.wait_ge(s_keyrow0, 16)
                    pick_rows(early, 0, keyrow0[:, :])
                if n == FIX + 5:
                    square_rows(early, 0)
                if STEP0 < n <= TIE:
                    raise_threshold(early, 0, n - STEP0 - 1)
                if STEP0 <= n < TIE:
                    count_candidates(early, 0, n - STEP0)
                if n == TIE:
                    count_ties(early, 0)
                if n == TIE + 1:
                    mask_rows(early, 0)
                if n == TIE + 3:
                    rows_turned(early, 0)
                if n == TIE + 9:
                    write_features(early, 0)
                    dve.memset(tmp[:, :], 0.0).then_inc(fixed_early, 1)
                for i, b in enumerate(ORDER):
                    if n == START[i] + AT_ADD:
                        add_features(i, b, routed, scale=(i == NB - 1))
                    if n == START[i] + AT_NORM:
                        normalise(i, b, routed)
                    if n == START[i] + AT_CHOOSE:
                        choose(i, b, routed)
                    if n == START[i] + AT_SECOND:
                        choose_second(i, b, routed)
                    if n == START[i] + AT_PROB:
                        probabilities(i, b, routed)
                    if n == START[i] + AT_ASSIGN:
                        assign(i, routed)

            dve.wait_ge(s_cnt, NB)
            link(dve.tensor_scalar(flags[:, :], count[:, :], float(TOPK), None, ALU.is_gt))
            dve.tensor_reduce(flagged[:, 0:1], flags[:, :], AX.X, ALU.add)
            dve.tensor_reduce(flagged[:, 1:2], flags[:, 0:SUB], AX.X, ALU.add).then_inc(s_flagged, 1)
            dve.wait_ge(s_nflags, 1)
            link(dve.tensor_copy(nflags[:, :], ps_flag[0:1, :]))
            link(dve.tensor_scalar(nflags[:, 1:2], nflags[:, 1:2], float(R), None, ALU.min))
            dve.tensor_tensor(redo_i[:, :], nflags[:, 0:1], nflags[:, 1:2], ALU.subtract).then_inc(s_redo, 1)

            redo = read_redo(dve)
            with dve.If(redo > 0):
                chain[:], before_if = [s_dve2, 0], chain[:]
                for i in range(2):
                    dve.wait_ge(routed.scat[i], NB // 2 * Q * 16)
                link(dve.tensor_copy(base[:, :], base_i[:, :]))
                dve.tensor_tensor(key[:, :], flags[:, :], rowidf[:, :], ALU.mult).then_inc(s_key, 1)
                dve.wait_ge(s_keyrow, 16)
                link(dve.tensor_scalar(keyflag, keyrow, 0.0, None, ALU.is_gt))
                link(dve.tensor_reduce(nflag[:, :], keyflag, AX.X, ALU.add))
                link(dve.tensor_scalar(nflag[:, :], nflag[:, :], 1.0 / R, 0.5 - 0.5 / R, ALU.mult, ALU.add))
                dve.tensor_scalar(nrounds[:, :], nflag[:, :], 1.0, None, ALU.max).then_inc(s_nr, 1)
                rounds = read_rounds(dve)
                with dve.Fori(0, rounds) as r:
                    pick_rows(general, r, keyrow)
                    square_rows(general, r)
                    for b in range(STEPS):
                        count_candidates(general, r, b)
                        raise_threshold(general, r, b)
                    count_ties(general, r)
                    mask_rows(general, r)
                    rows_turned(general, r)
                    write_features(general, r)
                dve.memset(tmp[:, :], 0.0).then_inc(s_fixed, 1)
                dve.wait_ge(s_fixed, 1)
                dve.wait_ge(s_xre, 16)
                for b in range(NB):
                    add_features(b, b, rerouted, scale=True)
                    normalise(b, b, rerouted)
                    choose(b, b, rerouted)
                    choose_second(b, b, rerouted)
                    probabilities(b, b, rerouted)
                    assign(b, rerouted)
                chain[:] = before_if

            dve.tensor_copy(pad_i[:, :], base[0:1, :]).then_inc(s_padr, 1)
            first = dve.tensor_tensor(tiles[:, :], base[0:1, :], base_i[0:1, :], ALU.subtract)
            link(first)
            link(dve.tensor_scalar(tiles_i[:, :], tiles[:, :], 1.0 / TS, 0.5 - 0.5 / TS, ALU.mult, ALU.add))
            link(dve.tensor_copy(tiles[:, :], tiles_i[:, :]))
            link(dve.tensor_tensor_scan(ends[:, :], ones_f[0:1, 0:E], tiles[:, :], 0.0, ALU.mult, ALU.add))
            dve.wait_ge(s_split, 4)
            link(dve.tensor_scalar(skip[:, :], tiles[:, :], -float(TS), float(RS), ALU.mult, ALU.add))
            TT = [1, NT + AHEAD, E]
            link(dve.tensor_tensor(past, tnum[:, :, :],
                                   ends[:, :].rearrange("p (o e) -> p o e", o=1).to_broadcast(TT), ALU.is_ge))
            link(dve.tensor_reduce(tile_e[:, :], past, AX.X, ALU.add))
            link(dve.tensor_tensor(jump, past,
                                   skip[:, :].rearrange("p (o e) -> p o e", o=1).to_broadcast(TT), ALU.mult))
            link(dve.tensor_reduce(tile_r[:, :], jump, AX.X, ALU.add))
            link(dve.scalar_tensor_tensor(tile_r[:, :], tnum[:, :, 0], float(TS), tile_r[:, :], ALU.mult, ALU.add))
            dve.tensor_scalar(tile_ei[:, :], tile_e[:, :], float(E - 1), None, ALU.min)
            dve.tensor_scalar(tile_ri[:, :], tile_r[:, :], float(E * RS), None, ALU.min).then_inc(s_tab, 1)

            def cut_x(t, q, fresh=False):
                dve.wait_ge(s_xh, t + 1)
                dve.tensor_tensor(xl[:, q, :], bank[4 + q][:, 0:TS], xh[:, q, :], ALU.subtract).then_inc(s_xlo, 1)

            def cut_h(t, q, fresh=False):
                if not fresh:
                    dve.wait_ge(s_y, t - 1)
                for half in range(2):
                    hb = slice(half * HB // 2, (half + 1) * HB // 2)
                    dve.wait_ge(s_relu, t * HB + (half + 1) * HB // 2)
                    dve.tensor_copy(hh[:, q, hb, :], relu[:, q, hb, :]).then_inc(s_hs, 1)
                    dve.wait_ge(s_hs, t * 4 + half * 2 + 1)
                    dve.tensor_tensor(hl[:, q, hb, :], relu[:, q, hb, :], hh[:, q, hb, :], ALU.subtract
                                      ).then_inc(s_hs, 1)

            cut_x(0, 0)
            cut_x(1, 1)
            for t in range(2):
                cut_h(t, t, fresh=True)
                cut_x(t + 2, t)
            with dve.Fori(1, NT // 2) as g:
                for u in range(2):
                    cut_h(g * 2 + u, u)
                    cut_x(g * 2 + u + 2, u)

            for g in range(NK):
                xb = xres[:, g * CK:(g + 1) * CK, :]
                dve.wait_ge(s_yl[g], 32)
                link(dve.tensor_tensor(xb, xb, yin[:, g, 0, :, :], ALU.add))
                dve.tensor_tensor(xb, xb, yin[:, g, 1, :, :], ALU.add).then_inc(s_sum, 1)

        @block.scalar
        def _(act):
            act.dma_start(wp_sb[:, :], w_proj).then_inc(s_w, 16)
            act.dma_start(wg_sb[:, :], w_gcn).then_inc(s_w, 16)
            act.dma_start(bp_sb[:, :], b_proj.rearrange("(p o) -> p o", o=1)).then_inc(s_w, 16)
            act.dma_start(bg_sb[:, :], b_gcn.rearrange("(p o) -> p o", o=1)).then_inc(s_w, 16)
            act.wait_ge(s_w, 64)
            act.activation(ex[:, 0:1], bp_sb[:, 0:1], ACT.Tanh)

            def tanh_chunk(n):
                act.wait_ge(s_sq, n + 1)
                if n >= NBUF:
                    act.wait_ge(s_pe, n - NBUF + 1)
                act.activation(tbuf[:, n % NBUF, :, :], abuf[:, n % NBUF, :, :], ACT.Tanh).then_inc(s_t, 1)

            for g in range(NK + 2):
                if g < NK:
                    act.wait_ge(s_tr, g + 1)
                    act.activation(xnorm_t[:, g * IW:(g + 1) * IW], [ps_x2, ps_xn][g % 2][:, :], ACT.Copy
                                   ).then_inc(s_trc, 1)
                if 1 <= g <= NK:
                    act.wait_ge(s_proj, g)
                    if g >= 3:
                        act.wait_ge(s_gp, g - 2)
                    act.activation(h2t[:, (g - 1) % 2, :], bank[6 + (g - 1) % 2][:, :], ACT.Tanh, bias=bp_sb[:, 0:1]
                                   ).then_inc(s_h2, 1)
                if g == NK:
                    tanh_chunk(0)
                if g >= 2:
                    act.wait_ge(s_gp, g - 1)
                    act.activation(g_sb[:, (g - 2) * CK:(g - 1) * CK, :],
                                   ps_feat[g % 2][:, :].rearrange("p (c d) -> p c d", c=CK), ACT.Copy
                                   ).then_inc(s_g, 1)

            def tanh_rows(f, r):
                act.wait_ge(f.rsq, r + 1)
                act.activation(rowval[:, :], rowval[:, :], ACT.Tanh).then_inc(f.val, 1)

            def features_out(f, r):
                act.wait_ge(f.fmm, r + 1)
                act.activation(fixrow[0:R, :], ps_fixrow, ACT.Copy).then_inc(f.frow, 1)

            def relu_rows(f, r):
                act.wait_ge(f.ft, r + 1)
                act.activation(fixed[:, :], ps_fixt[:, 0:R], ACT.Relu, bias=bg_sb[:, 0:1]).then_inc(f.fix, 1)

            def copy_norm(i, rs):
                q = i % 2
                act.wait_ge(rs.r2, i + 1)
                if i:
                    act.wait_ge(rs.r3, i)
                act.activation(xnt[:, :], ps_xn[:, :], ACT.Copy).then_inc(rs.xt, 1)
                if i >= 2:
                    act.wait_ge(rs.scat[q], i // 2 * Q * 16)
                act.activation(aug[:, q, 1, :, 0:D], aug[:, q, 0, :, 0:D], ACT.Copy).then_inc(rs.ax, 1)

            def exp_diff(i, rs):
                act.wait_ge(rs.df, i + 1)
                act.activation(ex[:, :], ex[:, :], ACT.Exp).then_inc(rs.ex, 1)

            def feat_out(ib):
                act.wait_ge(s_pe, (ib + 1) * NK)
                act.activation(feat_t[:, ib * IW:(ib + 1) * IW], ps_feat[ib % 2][:, :], ACT.Relu,
                               bias=bg_sb[:, 0:1]).then_inc(s_ev, 1)

            for n in range(END):
                if n < NCH:
                    if n:
                        tanh_chunk(n)
                if 0 < n <= NCH:
                    act.wait_ge(s_t, n)
                    act.activation(ind[:, (n - 1) % NBUF, :, :], tbuf[:, (n - 1) % NBUF, :, :], ACT.Sign
                                   ).then_inc(s_ind, 1)
                if n >= NK and n % NK == OUT:
                    if n // NK <= NB:
                        feat_out(n // NK - 1)
                if n == FIX:
                    act.wait_ge(s_key0, 1)
                    act.dma_start(keyrow0[:, :].rearrange("o (p t) -> o p t", p=P),
                                  key0[:, :].rearrange("p (o t) -> p o t", o=1)).then_inc(s_keyrow0, 16)
                if n == FIX + 3:
                    fetch_rows(act, early, 0)
                if n == FIX + 6:
                    tanh_rows(early, 0)
                if n == TIE + 6:
                    features_out(early, 0)
                if n == TIE + 8:
                    relu_rows(early, 0)
                for i in range(NB):
                    if n == START[i] + AT_COPY:
                        copy_norm(i, routed)
                    if n == START[i] + AT_EXP:
                        exp_diff(i, routed)

            redo = read_redo(act)
            with act.If(redo > 0):
                rounds = read_rounds(act)
                with act.Fori(0, rounds) as r:
                    tanh_rows(general, r)
                    features_out(general, r)
                    relu_rows(general, r)
                for b in range(NB):
                    copy_norm(b, rerouted)
                    exp_diff(b, rerouted)

            def upper_x(t, q, fresh=False):
                act.wait_ge(s_xp, t + 1)
                if not fresh:
                    act.wait_ge(s_h, (t - 1) * HB)
                act.activation(xh[:, q, :], bank[4 + q][:, 0:TS], ACT.Copy).then_inc(s_xh, 1)

            def relu_h(t, q, e, fresh=False):
                if not fresh:
                    act.wait_ge(s_hs, (t - 1) * 4)
                for hb in range(HB):
                    if hb % 2 == 0:
                        act.wait_ge(s_h, t * HB + hb + 2)
                    act.activation(relu[:, q, hb, :], bank[2 * q + hb // 2][:, hb % 2 * TS:(hb % 2 + 1) * TS],
                                   ACT.Relu, bias=b1_sb[:, bass.ds(e * HB + hb, 1)], scale=1.0 / WS
                                   ).then_inc(s_relu, 1)

            def y_out(t, u, q):
                act.wait_ge(s_y, t + 1)
                for s in range(2):
                    last = act.activation(ysb[:, u, s, :], bank[6 + q][:, s * D:(s + 1) * D], ACT.Copy,
                                          scale=xld[:, u, s, D + 1:D + 2])
                last.then_inc(s_yo, 1)

            act.wait_ge(s_tab, 1)
            upper_x(0, 0, fresh=True)
            upper_x(1, 1, fresh=True)

            def ffn_tiles(g, first):
                experts = load_experts(nc, act, g, NX)
                for u in range(NX):
                    t = g * NX + u
                    relu_h(t, u % 2, experts[u], fresh=first and u < 2)
                    upper_x(t + 2, u % 2)
                    if not (first and u == 0):
                        y_out(t - 1, (u - 1) % NX, (u - 1) % 2)

            ffn_tiles(0, True)
            with act.Fori(1, NT // NX) as g:
                ffn_tiles(g, False)
            y_out(NT - 1, NX - 1, (NX - 1) % 2)

            for g in range(NK):
                act.wait_ge(s_sum, g + 1)
                act.dma_start(out[g * IW:(g + 1) * IW, :].rearrange("(c p) d -> p c d", p=P),
                              xres[:, g * CK:(g + 1) * CK, :]).then_inc(s_out, 16)

        @block.tensor
        def _(pe):
            def transposes(src, dst, done):
                for cc in range(CK):
                    last = pe.transpose(dst[:, cc * P:(cc + 1) * P], src(cc), ident[:, :])
                last.then_inc(done, 1)

            pe.wait_ge(s_ident, 1)
            pe.wait_ge(s_w, 64)

            for g in range(NK + 2):
                if g < NK:
                    pe.wait_ge(s_xn1, g + 1)
                    if g >= 2:
                        pe.wait_ge(s_trc, g - 1)
                    transposes(lambda cc: xnorm[g * CK // HC][:, (g * CK + cc) % HC, :], [ps_x2, ps_xn][g % 2], s_tr)
                if 1 <= g <= NK:
                    pe.wait_ge(s_trc, g)
                    if g >= 3:
                        pe.wait_ge(s_h2, g - 2)
                    pe.matmul(bank[6 + (g - 1) % 2][:, :], wp_sb[:, :], xnorm_t[:, (g - 1) * IW:g * IW],
                              start=True, stop=True).then_inc(s_proj, 1)
                if g >= 2:
                    pe.wait_ge(s_h2, g - 1)
                    if g >= 4:
                        pe.wait_ge(s_g, g - 3)
                    for cc in range(CK):
                        last = pe.matmul(ps_feat[g % 2][:, cc * P:(cc + 1) * P],
                                         h2t[:, g % 2, cc * P:(cc + 1) * P], wg_sb[:, :], start=True, stop=True)
                    last.then_inc(s_gp, 1)
            pe.wait_ge(s_g, NK)
            pe.wait_ge(s_const, 1)

            TOTS = STEPS + 1

            def total_candidates(f, r, b):
                pe.wait_ge(f.part, r * TOTS + b + 1)
                pe.matmul(ps_ncand, same_row[:, :], ncand[:, :], start=True, stop=True).then_inc(f.tot, 1)

            def total_ties(f, r):
                pe.wait_ge(f.part, (r + 1) * TOTS)
                pe.matmul(ps_tie[:, 0:1], same_row[:, :], pair[:, 0:1], start=True, stop=True)
                pe.matmul(ps_tie[:, 1:2], before_row[:, :], pair[:, 1:2], start=True, stop=True
                          ).then_inc(f.tot, 1)

            def turn_rows(f, r):
                pe.wait_ge(f.keep, r + 1)
                pe.transpose(ps_rowt, rowgt[:, :], ident[:, :]).then_inc(f.rt, 1)

            def row_features(f, r, cs=range(C)):
                pe.wait_ge(f.rtc, r + 1)
                for c in cs:
                    last = pe.matmul(ps_fixrow, row_t[:, c::SEG], g_sb[:, c, :], start=(c == 0), stop=(c == C - 1))
                if cs[-1] == C - 1:
                    last.then_inc(f.fmm, 1)

            def turn_features(f, r):
                pe.wait_ge(f.frow, r + 1)
                pe.transpose(ps_fixt, fixrow[:, :], ident[:, :]).then_inc(f.ft, 1)

            def features_back(i, b, rs):
                if i:
                    pe.wait_ge(rs.x2, i)
                transposes(lambda cc: feat_t[:, (b * SUB + cc) * P:(b * SUB + cc + 1) * P], ps_x2, rs.r1)

            def normal_transpose(i, rs):
                pe.wait_ge(rs.xn, i + 1)
                if i:
                    pe.wait_ge(rs.xt, i)
                transposes(lambda cc: aug[:, i % 2, 0, cc, 0:D], ps_xn, rs.r2)

            def gate(i, rs):
                pe.wait_ge(rs.xt, i + 1)
                if i:
                    pe.wait_ge(rs.sl, i)
                for cc in range(SUB):
                    dst = ps_gate[:, cc * E:(cc + 1) * E]
                    last = pe.matmul(dst, xnt[:, cc * P:(cc + 1) * P], gate_w[:, :], start=True, stop=True)
                last.then_inc(rs.r3, 1)

            def places(i, rs):
                pe.wait_ge(rs.oh, i + 1)
                pe.matmul(ps_place, before[:, :], oh[:, :, :], start=True, stop=False, skip_group_check=True)
                for j in range(Q - 1):
                    n = Q - 1 - j
                    pe.matmul(ps_place[:, j + 1:, :], ones_bf[:, :],
                              oh[:, j:j + 1, :].to_broadcast([P, n, E]), start=False, stop=(j == Q - 2),
                              skip_group_check=True)
                for j in range(Q):
                    last = pe.matmul(ps_total, ones_bf[:, :], oh[:, j, :], start=(j == 0), stop=(j == Q - 1))
                last.then_inc(rs.r4, 1)

            for n in range(END):
                if n < NCH:
                    ib, k, buf = n // NK, n % NK, n % NBUF
                    if k == 0 and ib >= 2:
                        pe.wait_ge(s_ev, ib - 1)
                        pe.wait_ge(s_cnt, ib - 1)
                    pe.wait_ge(s_t, n + 1)
                    for cc in range(CK):
                        c = k * CK + cc
                        pe.matmul(ps_feat[ib % 2][:, :], g_sb[:, c, :], tbuf[:, buf, cc, :],
                                  start=(c == 0), stop=(c == C - 1))
                    pe.wait_ge(s_ind, n + 1)
                    for cc in range(CK):
                        c = k * CK + cc
                        for s in range(SUB):
                            last = pe.matmul(ps_cnt[ib % 2][:, s:s + 1], ind[:, buf, cc, s * P:(s + 1) * P],
                                             ones_bf[:, 0:1], start=(c == 0 and s == 0), stop=(c == C - 1),
                                             skip_group_check=True)
                    last.then_inc(s_pe, 1)
                if STEP0 <= n + 1 < TIE:
                    total_candidates(early, 0, n + 1 - STEP0)
                if n + 1 == TIE:
                    total_ties(early, 0)
                if n == TIE + 1:
                    turn_rows(early, 0)
                if n == TIE + 3:
                    row_features(early, 0, range(C // 2))
                if n == TIE + 4:
                    row_features(early, 0, range(C // 2, C))
                if n == TIE + 6:
                    turn_features(early, 0)
                for i, b in enumerate(ORDER):
                    if n == START[i]:
                        pe.wait_ge(s_ev, b + 1)
                        if i == 0:
                            pe.wait_ge(s_small, 80)
                        if b == 0:
                            pe.wait_ge(fixed_early, 1)
                        features_back(i, b, routed)
                    if n == START[i] + AT_TURN:
                        normal_transpose(i, routed)
                    if n == START[i] + AT_GATE:
                        gate(i, routed)
                    if n == START[i] + AT_PLACE:
                        places(i, routed)
            pe.wait_ge(s_flagged, 1)
            pe.matmul(ps_flag, ones_bf[:, :], flagged[:, :], start=True, stop=True).then_inc(s_nflags, 1)

            redo = read_redo(pe)
            with pe.If(redo > 0):
                rounds = read_rounds(pe)
                with pe.Fori(0, rounds) as r:
                    for b in range(STEPS):
                        total_candidates(general, r, b)
                    total_ties(general, r)
                    turn_rows(general, r)
                    row_features(general, r)
                    turn_features(general, r)
                pe.wait_ge(s_fixed, 1)
                for b in range(NB):
                    features_back(b, b, rerouted)
                    normal_transpose(b, rerouted)
                    gate(b, rerouted)
                    places(b, rerouted)

            pe.wait_ge(s_split, 4)
            pe.wait_ge(s_tab, 1)

            def turn_x(t, u, fresh=False, round_=0):
                pe.wait_ge(s_xl[u], round_ * 16 + 16)
                if not fresh:
                    pe.wait_ge(s_xlo, t - 1)
                for s in range(2):
                    last = pe.transpose(bank[4 + u % 2][:, s * P:(s + 1) * P], xld[:, u, s, 0:D], ident[:, :])
                last.then_inc(s_xp, 1)

            def layer1(t, q, e, fresh=False):
                pe.wait_ge(s_xlo, t + 1)
                for hb in range(HB):
                    if not fresh and hb % 2 == 0:
                        pe.wait_ge(s_relu, (t - 2) * HB + hb + 2)
                    dst = bank[2 * q + hb // 2][:, hb % 2 * TS:(hb % 2 + 1) * TS]
                    hi = w1h[:, bass.ds(e, 1), hb * P:(hb + 1) * P].rearrange("p o h -> p (o h)")
                    lo = w1l[:, bass.ds(e, 1), hb * P:(hb + 1) * P].rearrange("p o h -> p (o h)")
                    pe.matmul(dst, hi, xh[:, q, :], start=True, stop=False)
                    pe.matmul(dst, hi, xl[:, q, :], start=False, stop=False)
                    pe.matmul(dst, lo, xh[:, q, :], start=False, stop=True).then_inc(s_h, 1)

            def layer2(t, q, e, fresh=False):
                if not fresh:
                    pe.wait_ge(s_yo, t - 1)
                for hb in range(HB):
                    if hb % 2 == 0:
                        pe.wait_ge(s_hs, t * 4 + hb + 2)
                    hi = w2h[:, bass.ds(e, 1), hb, :].rearrange("p o d -> p (o d)")
                    lo = w2l[:, bass.ds(e, 1), hb, :].rearrange("p o d -> p (o d)")
                    for s in range(2):
                        dst = bank[6 + q][:, s * D:(s + 1) * D]
                        hs, ls = hh[:, q, hb, s * P:(s + 1) * P], hl[:, q, hb, s * P:(s + 1) * P]
                        pe.matmul(dst, hs, hi, start=(hb == 0 and s == 0), stop=False, skip_group_check=True)
                        pe.matmul(dst, hs, lo, start=False, stop=False, skip_group_check=True)
                        pe.matmul(dst, ls, hi, start=False, stop=False, skip_group_check=True)
                for s in range(2):
                    last = pe.matmul(bank[6 + q][:, s * D:(s + 1) * D], ones_h[:, :],
                                     b2_hl[:, bass.ds(e, 1), :].rearrange("p o d -> p (o d)"),
                                     start=False, stop=True, skip_group_check=True)
                last.then_inc(s_y, 1)

            turn_x(0, 0, fresh=True)
            turn_x(1, 1, fresh=True)
            layer1(0, 0, pe.value_load(tile_ei[0:1, 0:1], min_val=0, max_val=E - 1), fresh=True)

            def ffn_tiles(g, first):
                experts = load_experts(nc, pe, g, NX + 1)
                for u in range(NX):
                    t = g * NX + u
                    turn_x(t + 2, (u + 2) % NX, round_=g + (u + 2) // NX)
                    layer1(t + 1, (u + 1) % 2, experts[u + 1], fresh=first and u < 1)
                    layer2(t, u % 2, experts[u], fresh=first and u < 2)

            ffn_tiles(0, True)
            with pe.Fori(1, NT // NX) as g:
                ffn_tiles(g, False)


def kernel(**inputs):
    import concourse.bacc as bacc
    from concourse.bass_utils import run_bass_kernel_spmd

    a = {k: np.asarray(v) for k, v in inputs.items()}
    adj = a["adj"]
    N = adj.shape[0]
    C = N // P
    w1, w2, b1 = a["L0_ffn_W1"], a["L0_ffn_W2"], a["L0_ffn_b1"]
    E, H, D = w1.shape
    laid = {
        "x": a["x"],
        "adj_tiles": adj.reshape(N // IW, IW, C // CK, CK, P).transpose(0, 2, 4, 3, 1),
        "adj_rows": adj,
        "w_proj": a["L0_gnn_W_proj"], "b_proj": a["L0_gnn_b_proj"],
        "w_gcn": a["L0_gnn_W_gcn"], "b_gcn": a["L0_gnn_b_gcn"],
        "w_gate": a["L0_ffn_Wg"].T, "b_gate": a["L0_ffn_bg"],
        "w1": w1.transpose(2, 0, 1),
        "b1": b1.reshape(E * (H // P), P).T,
        "w2": w2.reshape(E, D, H // P, P).transpose(3, 0, 2, 1),
        "b2": a["L0_ffn_b2"],
    }
    nc = bacc.Bacc("TRN2", target_bir_lowering=False, num_devices=1)
    arrays, args = {}, []
    for name, v in laid.items():
        v = np.ascontiguousarray(v)
        arrays["in_" + name] = v
        args.append(nc.dram_tensor("in_" + name, v.shape, mybir.dt.from_np(v.dtype), kind="ExternalInput").ap())
    res = nc.dram_tensor("out_0", a["x"].shape, mybir.dt.float32, kind="ExternalOutput").ap()
    gnn_moe_layer(nc, *args, res)
    r = run_bass_kernel_spmd(nc, [arrays], core_ids=[0])
    return r.results[0]["out_0"]
```
